# Optimizing a Trainium2 kernel written in Bass

```python
import numpy as np
import jax
import jax.numpy as jnp

def _softmax(x, axis=-1):
    return jax.nn.softmax(x, axis=axis)

def _gelu(x):
    return jax.nn.gelu(x, approximate=True)

def _silu(x):
    return jax.nn.silu(x)

def _sigmoid(x):
    return jax.nn.sigmoid(x)

def _layernorm(x, axis=-1, eps=1e-05):
    m = jnp.mean(x, axis=axis, keepdims=True)
    v = jnp.var(x, axis=axis, keepdims=True)
    return (x - m) / jnp.sqrt(v + eps)

def _scatter_add(tgt, idx, src, axis=0):
    return tgt.at[idx].add(src)

def _segment_sum(src, seg, n):
    return jax.ops.segment_sum(src, seg, n)
kernel_name = 'mk_flamingo_gated_d1_seqx_r4_5eb448'

def setup_inputs(seed: int=0):
    np.random.seed(seed)
    _w = jnp.asarray

    def _rec_inputs():
        import jax
        import jax.numpy as jnp
        _rk = jax.random.key(seed)
        x = -0.0002928 + 1 * jax.random.normal(jax.random.fold_in(_rk, 1), (16, 128, 512), jnp.float32)
        _lenS = 128 - jax.random.randint(jax.random.fold_in(_rk, 7), (16,), 0, max(1, 128 // 4) + 1, jnp.int32)
        _lenS2 = 128 - jax.random.randint(jax.random.fold_in(_rk, 8), (16,), 0, max(1, 128 // 4) + 1, jnp.int32)
        _ctx_2048P = jax.random.normal(jax.random.fold_in(_rk, 11), (16, 16, 512), jnp.float32)
        _ctx_2048c = jax.random.dirichlet(jax.random.fold_in(_rk, 511), 0.3 * jnp.ones((16,), jnp.float32), (16, 128))
        _ctx_2048t = jnp.einsum('bsk,bkd->bsd', _ctx_2048c, _ctx_2048P)
        _ctx_2048t = _ctx_2048t * jax.lax.rsqrt(jnp.mean(jnp.square(_ctx_2048t)) + 1e-12) * 0.953939
        ctx_2048 = -1.39393e-06 + 0.999914 * (_ctx_2048t + 0.3 * jax.random.normal(jax.random.fold_in(_rk, 611), (16, 128, 512), jnp.float32))
        _g = jax.random.normal(jax.random.fold_in(_rk, 9001), (2, 1), jnp.float32)
        _g = jnp.sign(_g) * jnp.maximum(jnp.abs(_g), 1.0) + (_g == 0) * 1.0
        g_xattn = _g[0]
        g_ffn = _g[1]
        return (x, ctx_2048, g_xattn, g_ffn)
    x, ctx_2048, g_xattn, g_ffn = _rec_inputs()

    def _L0_xattn_setup():
        import math
        import jax, jax.numpy as jnp
        import numpy as np
        N_HEADS = 8
        CHANNELS = 128
        K_CH = CHANNELS // N_HEADS
        THETA = 10000.0

        def _rope_freqs(length, dim):
            inv_freq = 1.0 / THETA ** (jnp.arange(0, dim, 2, dtype=jnp.float32) / dim)
            f = jnp.arange(length, dtype=jnp.float32)[:, None] * inv_freq[None, :]
            return jnp.concatenate([f, f], axis=-1)

        def _apply_rotary(pos, t):
            half = t.shape[-1] // 2
            rot = jnp.concatenate([-t[..., half:], t[..., :half]], axis=-1)
            return t * jnp.cos(pos) + rot * jnp.sin(pos)

        def _proj(inp, W, b):
            return jnp.einsum('oc,bct->bot', W, inp) + b[None, :, None]
        key = jax.random.key(seed)
        ks = jax.random.split(key, 10)
        B, C, T = (4, CHANNELS, 512)
        bound = math.sqrt(6.0 / (C + C))

        def w(k):
            return jax.random.uniform(k, (C, C), jnp.float32, -bound, bound)
        return {'x': jax.random.normal(ks[0], (B, C, T), jnp.float32), 'c': jax.random.normal(ks[1], (B, C, T), jnp.float32), 'Wq': w(ks[2]), 'bq': jnp.zeros((C,), jnp.float32), 'Wk': w(ks[3]), 'bk': jnp.zeros((C,), jnp.float32), 'Wv': w(ks[4]), 'bv': jnp.zeros((C,), jnp.float32), 'Wo': w(ks[5]), 'bo': jnp.zeros((C,), jnp.float32)}
    _L0_xattn_all = _L0_xattn_setup()
    _L0_xattn_in = {k: v for k, v in _L0_xattn_all.items() if k in ('Wq', 'bq', 'Wk', 'bk', 'Wv', 'bv', 'Wo', 'bo')}
    del _L0_xattn_all

    def _L0_ffn_setup():
        import jax, jax.numpy as jnp
        import numpy as np
        D_MODEL = 512
        D_EXPERT = 2048
        EPS = 1e-08

        def ternary_quant(w):
            scale = jnp.mean(jnp.abs(w)) + EPS
            q = jnp.clip(jnp.round(w / scale), -1.0, 1.0) * scale
            return w + jax.lax.stop_gradient(q - w)
        key = jax.random.key(seed)
        k_x, k_up, k_gate, k_down = jax.random.split(key, 4)
        std_in = 1.0 / np.sqrt(D_MODEL)
        std_exp = 1.0 / np.sqrt(D_EXPERT)
        return {'x': jax.random.normal(k_x, (4, 512, D_MODEL), dtype=jnp.float32), 'W_up': jax.random.normal(k_up, (D_EXPERT, D_MODEL), dtype=jnp.float32) * std_in, 'W_gate': jax.random.normal(k_gate, (D_EXPERT, D_MODEL), dtype=jnp.float32) * std_in, 'W_down': jax.random.normal(k_down, (D_MODEL, D_EXPERT), dtype=jnp.float32) * std_exp}
    _L0_ffn_all = _L0_ffn_setup()
    _L0_ffn_in = {k: v for k, v in _L0_ffn_all.items() if k in ('W_up', 'W_gate', 'W_down')}
    del _L0_ffn_all
    return {'x': x, 'ctx_2048': ctx_2048, 'g_xattn': g_xattn, 'g_ffn': g_ffn, 'L0_xattn_Wq': _L0_xattn_in['Wq'], 'L0_xattn_bq': _L0_xattn_in['bq'], 'L0_xattn_Wk': _L0_xattn_in['Wk'], 'L0_xattn_bk': _L0_xattn_in['bk'], 'L0_xattn_Wv': _L0_xattn_in['Wv'], 'L0_xattn_bv': _L0_xattn_in['bv'], 'L0_xattn_Wo': _L0_xattn_in['Wo'], 'L0_xattn_bo': _L0_xattn_in['bo'], 'L0_ffn_W_up': _L0_ffn_in['W_up'], 'L0_ffn_W_gate': _L0_ffn_in['W_gate'], 'L0_ffn_W_down': _L0_ffn_in['W_down']}

def reference(x, ctx_2048, g_xattn, g_ffn, L0_xattn_Wq, L0_xattn_bq, L0_xattn_Wk, L0_xattn_bk, L0_xattn_Wv, L0_xattn_bv, L0_xattn_Wo, L0_xattn_bo, L0_ffn_W_up, L0_ffn_W_gate, L0_ffn_W_down):
    import jax
    import jax.numpy as jnp

    def _L0_xattn_ref(x, c, Wq, bq, Wk, bk, Wv, bv, Wo, bo):
        import math
        import jax, jax.numpy as jnp
        import numpy as np
        N_HEADS = 8
        CHANNELS = 128
        K_CH = CHANNELS // N_HEADS
        THETA = 10000.0

        def _rope_freqs(length, dim):
            inv_freq = 1.0 / THETA ** (jnp.arange(0, dim, 2, dtype=jnp.float32) / dim)
            f = jnp.arange(length, dtype=jnp.float32)[:, None] * inv_freq[None, :]
            return jnp.concatenate([f, f], axis=-1)

        def _apply_rotary(pos, t):
            half = t.shape[-1] // 2
            rot = jnp.concatenate([-t[..., half:], t[..., :half]], axis=-1)
            return t * jnp.cos(pos) + rot * jnp.sin(pos)

        def _proj(inp, W, b):
            return jnp.einsum('oc,bct->bot', W, inp) + b[None, :, None]
        b, _, t_t = x.shape
        t_s = c.shape[2]
        q_emb = _rope_freqs(t_t, K_CH)
        k_emb = _rope_freqs(t_s, K_CH)

        def split_heads(t):
            return t.reshape(b, N_HEADS, K_CH, t.shape[2]).transpose(0, 1, 3, 2)
        q = split_heads(_proj(x, Wq, bq))
        k = split_heads(_proj(c, Wk, bk))
        v = split_heads(_proj(c, Wv, bv))
        q = _apply_rotary(q_emb, q)
        k = _apply_rotary(k_emb, k)
        scores = jnp.einsum('bhtc,bhsc->bhts', q, k) / math.sqrt(K_CH)
        p_attn = jax.nn.softmax(scores, axis=-1)
        out = jnp.einsum('bhts,bhsc->bhtc', p_attn, v)
        out = out.transpose(0, 1, 3, 2).reshape(b, N_HEADS * K_CH, t_t)
        return _proj(out, Wo, bo)

    def _L0_ffn_ref(x, W_up, W_gate, W_down):
        import jax, jax.numpy as jnp
        import numpy as np
        D_MODEL = 512
        D_EXPERT = 2048
        EPS = 1e-08

        def ternary_quant(w):
            scale = jnp.mean(jnp.abs(w)) + EPS
            q = jnp.clip(jnp.round(w / scale), -1.0, 1.0) * scale
            return w + jax.lax.stop_gradient(q - w)
        wu = ternary_quant(W_up)
        wg = ternary_quant(W_gate)
        wd = ternary_quant(W_down)
        up = jnp.einsum('bsd,ed->bse', x, wu)
        gate = jnp.einsum('bsd,ed->bse', x, wg)
        hidden = jax.nn.silu(up) * gate
        return jnp.einsum('bse,de->bsd', hidden, wd)
    x = x + jnp.tanh(g_xattn[0]) * _L0_xattn_ref(_layernorm(x, axis=-1), ctx_2048, L0_xattn_Wq, L0_xattn_bq, L0_xattn_Wk, L0_xattn_bk, L0_xattn_Wv, L0_xattn_bv, L0_xattn_Wo, L0_xattn_bo)
    x = x + jnp.tanh(g_ffn[0]) * _L0_ffn_ref(_layernorm(x, axis=-1), L0_ffn_W_up, L0_ffn_W_gate, L0_ffn_W_down)
    return x

_drawn_inputs = setup_inputs


def setup_inputs(seed=0):
    import zlib

    import numpy as np

    out = dict(_drawn_inputs(seed))
    spreads = {'L0_xattn_bq': (0.0, 0.431),
     'L0_xattn_bk': (0.0, 0.8),
     'L0_xattn_bv': (0.0, 0.1),
     'L0_xattn_bo': (0.0, 0.1)}
    factors = {}
    for name, (base, spread) in spreads.items():
        noise = np.random.default_rng([zlib.crc32(name.encode()), seed]).standard_normal(out[name].shape)
        drawn = base * np.exp(spread * noise) if base else spread * noise
        out[name] = jnp.asarray(drawn.astype(out[name].dtype))
    for name, factor in factors.items():
        out[name] = (out[name] * factor).astype(out[name].dtype)
    return out
```

```python
import numpy as np
import concourse.bass as bass
from concourse import mybir
from contextlib import ExitStack

BATCH, CH, SEQ = 16, 128, 512
HEADS = 8
HD = CH // HEADS
EXPERT = 2048
P = 128
TT = SEQ // P
ET = EXPERT // P
GROUP = HEADS // 2
PAIR = 2
PAIRS = BATCH // PAIR
TILES = HEADS * TT
QUADS = TILES // GROUP
QK_SCALE = 16.0
SHIFT = QK_SCALE * QK_SCALE
XN_SCALE = 2048.0
HID_SCALE = 16.0
LAG = 6
SHIFT_ROW = 96
LN_EPS = 1e-5
TERNARY_EPS = 1e-8

S_OT1, S_OBACK, S_ROW1, S_WO = 4, 7, 8, 9
S_QPROJ, S_KPROJ, S_VPROJ, S_XT0, S_XT1, S_OT0, S_ROW0 = 11, 13, 15, 17, 19, 22, 24
S_FFN = 20


def flamingo_block(nc, x, ctxt, g_xattn, g_ffn, wqT, bq, wkT, bk, wvT, bv, woT, bo,
                   wupT, wgateT, wdownT, cos, sin, out):
    f32, f16 = mybir.dt.float32, mybir.dt.float16
    ALU, ACT, AX = mybir.AluOpType, mybir.ActivationFunctionType, mybir.AxisListType

    ctx = ExitStack()
    with ctx:
        def sb(name, shape, dt=f32):
            return ctx.enter_context(nc.sbuf_tensor(name, shape, dt))

        def sem(name):
            return ctx.enter_context(nc.semaphore(name))

        arena = sb("arena", [P, 16384])
        stage_a = arena[:, 0:8192]
        stage_b = arena[:, 8192:16384]
        w_up = sb("w_up", [P, TT, EXPERT], f16)
        w_gate = sb("w_gate", [P, TT, EXPERT], f16)
        w_down = arena[:, 12288:16384].bitcast(f16).rearrange("p (t d) -> p t d", t=ET)
        hid = arena[:, 0:4096].bitcast(f16).rearrange("p (e l r) -> p e l r", e=ET, l=2)
        x1_res = arena[:, 4096:5120].rearrange("p (b t) -> p b t", b=PAIR)
        y_out = arena[:, 5120:6144].rearrange("p (b t) -> p b t", b=PAIR)
        xT = arena[:, 6144:7168].bitcast(f16).rearrange("p (t l r) -> p t l r", t=TT, l=2)
        th = arena[:, 7168:7680].rearrange("p (b r) -> p b r", b=2)
        hu = arena[:, 7680:7936]
        hb = arena[:, 7936:8448].rearrange("p (b r) -> p b r", b=2)

        q_st = [sb(f"q_st{i}", [P, HEADS, SEQ], f16) for i in range(2)]
        k_st = [sb(f"k_st{i}", [P, HEADS, SEQ], f16) for i in range(2)]
        probs = sb("probs", [P, 2 * GROUP, SEQ])
        xin = [sb(f"xin{i}", [P, SEQ]) for i in range(2)]
        cin = [sb(f"cin{i}", [P, SEQ]) for i in range(2)]
        xres = [sb(f"xres{i}", [P, SEQ]) for i in range(2)]
        cos_sb, sin_sb = sb("cos_sb", [P, SEQ]), sb("sin_sb", [P, SEQ])
        qb, kb, rq, rk = (sb(n, [P, SEQ]) for n in ("qb", "kb", "rq", "rk"))
        q_hl, k_hl = sb("q_hl", [P, 2, SEQ], f16), sb("k_hl", [P, 2, SEQ], f16)
        v_sb = [sb(f"v_sb{i}", [P, TT, HEADS, 2 * HD]) for i in range(2)]
        o_raw = sb("o_raw", [P, 2, SEQ])
        o_tok = sb("o_tok", [P, TT, CH])
        o_ch = sb("o_ch", [P, SEQ])
        attn = sb("attn", [P, SEQ])
        x1 = sb("x1", [P, PAIR, SEQ])
        xn2 = sb("xn2", [P, SEQ])
        x_hl = [sb(f"x_hl{i}", [P, 2, SEQ], f16) for i in range(2)]
        wq_sb, wk_sb, wv_sb, wo_sb, bv_sb = (sb(n, [P, CH]) for n in ("wq_sb", "wk_sb", "wv_sb", "wo_sb", "bv_sb"))
        ident = sb("ident", [P, P])
        ident16 = sb("ident16", [P, P], f16)
        ones = sb("ones", [P, P])
        maxima = sb("maxima", [P, TILES])
        max16 = sb("max16", [P, TILES], f16)
        max_row = [sb(f"max_row{i}", [16, P], f16) for i in range(2)]
        rec = sb("rec", [P, 2, 16])
        stats1, mv1, stats2, mv2 = sb("stats1", [P, 6]), sb("mv1", [P, 2]), sb("stats2", [P, 6]), sb("mv2", [P, 2])
        ve1, rstd1, ve2, rstd2, rstd2s = (sb(n, [P, 1]) for n in ("ve1", "rstd1", "ve2", "rstd2", "rstd2s"))
        half_neg = sb("half_neg", [P, 1])
        gates = sb("gates", [P, 2])
        tgate = sb("tgate", [P, 2])
        biases = sb("biases", [P, 3])
        bq16, bk16, tbo = sb("bq16", [P, 1]), sb("bk16", [P, 1]), sb("tbo", [P, 1])
        asum = sb("asum", [P, 3, 4])
        wscale = sb("wscale", [P, 3])
        wsum = sb("wsum", [P, 3])
        thr, nthr = sb("thr", [P, 3]), sb("nthr", [P, 3])
        up_half = sb("up_half", [P, 1])
        yc1, yc2, y_coef = sb("yc1", [P, 1]), sb("yc2", [P, 1]), sb("y_coef", [P, 1])

        q_scr = nc.dram_tensor("q_scr", [2, P, SEQ], f16, kind="Internal").ap()
        k_scr = nc.dram_tensor("k_scr", [2, P, SEQ], f16, kind="Internal").ap()

        def bank(name):
            return ctx.enter_context(nc.psum_tensor(name, [P, 512], f32))

        st_ps = [bank("st_ps0"), bank("st_ps1")]
        mx_ps = [bank("mx_ps0"), bank("mx_ps1")]
        pv_ps = bank("pv_ps")
        misc = bank("misc")
        ff_ps = [bank("ff_ps0"), bank("ff_ps1")]
        misc16 = misc[:, :].bitcast(f16)

        consts_set, ident_set = sem("consts_set"), sem("ident_set")
        small_loaded, small_ready, dve_small = sem("small_loaded"), sem("small_ready"), sem("dve_small")
        gate_tanh = sem("gate_tanh")
        up_loaded, gate_loaded, down_loaded = sem("up_loaded"), sem("gate_loaded"), sem("down_loaded")
        w_loaded = [up_loaded, gate_loaded, down_loaded]
        abs_done, wsum_ready, wscale_done = sem("abs_done"), sem("wsum_ready"), sem("wscale_done")
        quant_low, quant_done = sem("quant_low"), sem("quant_done")
        xin_loaded = [sem("xin_loaded0"), sem("xin_loaded1")]
        cin_loaded = [sem("cin_loaded0"), sem("cin_loaded1")]
        xres_loaded = [sem("xres_loaded0"), sem("xres_loaded1")]
        bn1_done, mv1_done, ve1_done, rstd1_done, xn_done = (sem(n) for n in ("bn1_done", "mv1_done", "ve1_done", "rstd1_done", "xn_done"))
        q_ready, k_ready, v_ready = sem("q_ready"), sem("k_ready"), sem("v_ready")
        qb_done, kb_done, v_done = sem("qb_done"), sem("kb_done"), sem("v_done")
        rq_done, rk_done = sem("rq_done"), sem("rk_done")
        rope_q, rope_k = sem("rope_q"), sem("rope_k")
        qhi_done, khi_done, qlo_done, klo_done = (sem(n) for n in ("qhi_done", "khi_done", "qlo_done", "klo_done"))
        scr_written = sem("scr_written")
        st_loaded = [sem("st_loaded0"), sem("st_loaded1")]
        mx_ready, mx_done, max16_done, maxT_ready, max_row_done = (sem(n) for n in ("mx_ready", "mx_done", "max16_done", "maxT_ready", "max_row_done"))
        row_loaded = [sem("row_loaded0"), sem("row_loaded1")]
        st_ready, exp_done, pv_done, o_copied = (sem(n) for n in ("st_ready", "exp_done", "pv_done", "o_copied"))
        oT_ready, rec_done, o_tok_done, ob_ready, o_ch_done = (sem(n) for n in ("oT_ready", "rec_done", "o_tok_done", "ob_ready", "o_ch_done"))
        wo_ready, attn_done, x1_done = sem("wo_ready"), sem("attn_done"), sem("x1_done")
        bn2_done, mv2_done, rstd2_step, xn2_done, xhi_done, xlo_done = (sem(n) for n in ("bn2_done", "mv2_done", "rstd2_step", "xn2_done", "xhi_done", "xlo_done"))
        xT_ready, xT_done = sem("xT_ready"), sem("xT_done")
        ug_ready, tanh_done, hu_done, hb_done, hhi_done, hlo_done = (sem(n) for n in ("ug_ready", "tanh_done", "hu_done", "hb_done", "hhi_done", "hlo_done"))
        x1_moved, y_ready, y_done = sem("x1_moved"), sem("y_ready"), sem("y_done")
        out_written = [sem("out_written0"), sem("out_written1")]
        passed = sem("passed")
        block = ctx.enter_context(nc.Block())

        def wait(eng, s, value, total=None):
            if isinstance(value, int):
                if total is not None:
                    value = min(value, total)
                if value <= 0:
                    return
            eng.wait_ge(s, value)

        def carry_wait(eng):
            eng.sem_inc(passed, 1)

        def exists(b, count=BATCH):
            return not isinstance(b, int) or 0 <= b < count

        def is_at(b, n):
            return isinstance(b, int) and b == n

        def pairs(eng, iteration, last=PAIRS - 2):
            for p in (-1, 0, 1):
                for e in range(PAIR):
                    iteration(p, e)
            with eng.Fori(2, last + 1) as p:
                for e in range(PAIR):
                    iteration(p, e)
            for p in range(last + 1, PAIRS + 2):
                for e in range(PAIR):
                    iteration(p, e)

        def up_gate_span(S):
            n = 6 * (S - S_FFN)
            return range(max(n, 0), max(min(n + 6, 16 * ET), 0))

        def ffn_tile_at(S):
            done = [n // 16 for n in up_gate_span(S) if n % 16 == 15]
            return done[0] if done else None

        @block.tensor
        def _(pe):
            MM, TR = nc.tensor.matmul, nc.tensor.transpose

            def weight_sum(m):
                pe.wait_ge(abs_done, 4 * (m + 1))
                if m:
                    pe.wait_ge(wscale_done, m)
                MM(ff_ps[0][:, 0:4], ones[:, :], asum[:, m, :], start=True, stop=True).then_inc(wsum_ready, 1)

            def iteration(p, e):
                b = PAIR * p + e
                for s in range(TILES):
                    S = TILES * e + s
                    if exists(b):
                        if s == 0:
                            wait(pe, row_loaded[0], 16 * (b + 1))
                        if s == TILES // 2:
                            wait(pe, row_loaded[1], 16 * (b + 1))
                        h, j = GROUP * (s // 16) + s % 4, (s % 16) // 4
                        wait(pe, exp_done, TILES * b + s - 1)
                        MM(st_ps[s % 2][:, :], k_st[e][:, h, P * j:P * j + P], q_st[e][:, h, :],
                           start=True, stop=True).then_inc(st_ready, 1)
                    mb, m = (b, s + TILES - LAG) if s < LAG else (b + 1, s - LAG)
                    me = e if s < LAG else 1 - e
                    if exists(mb):
                        if m == 0:
                            wait(pe, st_loaded[me], 128 * (p + 2 if e else p + 1))
                        h, j = m // TT, m % TT
                        wait(pe, mx_done, TILES * mb + m - 1)
                        MM(mx_ps[m % 2][:, :], q_st[me][0:SHIFT_ROW, h, P * j:P * j + P],
                           k_st[me][0:SHIFT_ROW, h, :], start=True, stop=True).then_inc(mx_ready, 1)
                    if exists(p - 1, PAIRS):
                        for n in up_gate_span(S):
                            t, r = n // 16, n % 16
                            if n == 0:
                                wait(pe, xT_done, 2 * p)
                                if is_at(p, 1):
                                    pe.wait_ge(quant_done, 24)
                            if n == 0:
                                wait(pe, y_done, 2 * (p - 1) - 1)
                            if n == 16:
                                wait(pe, y_done, 2 * (p - 1))
                            if r == 0:
                                wait(pe, hb_done, ET * (p - 1) + t - 1)
                            w, c = (w_up, 0) if r < 8 else (w_gate, 256)
                            k, hl = (r % 8) // 2, r % 2
                            mm = MM(ff_ps[t % 2][:, c:c + 256], w[:, k, P * t:P * t + P], xT[:, k, hl, :],
                                    start=(r % 8 == 0), stop=(r % 8 == 7))
                            if r == 15:
                                mm.then_inc(ug_ready, 1)
                    if exists(p - 2, PAIRS) and S < 16:
                        for n in range(4 * S, 4 * S + 4):
                            i, t, hl = n // 32, (n % 32) // 2, n % 2
                            if n % 32 == 0:
                                wait(pe, hb_done, ET * (p - 1))
                            if i == 0 and hl == 0:
                                wait(pe, hlo_done, ET * (p - 2) + t + 1)
                            mm = MM(ff_ps[i][:, :], hid[:, t, hl, P * i:P * i + P], w_down[:, t, :],
                                    start=(n % 32 == 0), stop=(n % 32 == 31))
                        if n % 32 == 31:
                            mm.then_inc(y_ready, 1)
                    qb_, k = (b, (s - 5) // 4) if s >= 5 else (b - 1, QUADS - 1)
                    if s % 4 == 1 and exists(qb_):
                        ve = e if s >= 5 else 1 - e
                        g, j = k // 4, k % 4
                        wait(pe, exp_done, TILES * qb_ + 4 * k + 4)
                        if k == 0:
                            wait(pe, v_done, qb_ + 1)
                        if k % 4 == 0:
                            wait(pe, o_copied, 2 * qb_ + g)
                        for a in range(GROUP):
                            mm = MM(pv_ps[32 * a:32 * a + 32, :], v_sb[ve][:, j, GROUP * g + a, :],
                                    probs[:, (4 * k + a) % 8, :], start=(j == 0), stop=(j == TT - 1))
                        mm.then_inc(pv_done, 1)
                    if (s == S_OT1 and exists(b - 1)) or (s == S_OT0 and exists(b)):
                        ob, g = (b - 1, 1) if s == S_OT1 else (b, 0)
                        wait(pe, o_copied, 2 * ob + g + 1)
                        if g:
                            wait(pe, o_tok_done, 2 * ob + g)
                            wait(pe, max_row_done, 2 * (ob + 1) + 1, 2 * BATCH)
                        else:
                            wait(pe, v_done, b + 2, BATCH)
                            wait(pe, attn_done, b)
                            if e == 0:
                                wait(pe, xT_done, 2 * p)
                        for j in range(TT):
                            mm = TR(misc[:, P * j:P * j + P], o_raw[:, g, P * j:P * j + P], ident[:, :])
                        mm.then_inc(oT_ready, 1)
                    if s == S_OBACK and exists(b - 1):
                        wait(pe, o_tok_done, 2 * b)
                        for j in range(TT):
                            mm = TR(misc[:, P * j:P * j + P], o_tok[:, j, :], ident[:, :])
                        mm.then_inc(ob_ready, 1)
                    if (s == S_ROW1 and exists(b)) or (s == S_ROW0 and exists(b + 1)):
                        rb, half = (b, 1) if s == S_ROW1 else (b + 1, 0)
                        wait(pe, max16_done, 2 * rb + half + 1)
                        if half:
                            wait(pe, o_ch_done, b)
                            wait(pe, max_row_done, 2 * b + 1)
                        else:
                            wait(pe, o_tok_done, 2 * b + 1)
                            wait(pe, v_done, b + 2, BATCH)
                        TR(misc16[0:16, 0:P], max16[:, 16 * half:16 * half + 16], ident16[:, :]).then_inc(maxT_ready, 1)
                    if s == S_WO and exists(b - 1):
                        wait(pe, o_ch_done, b)
                        wait(pe, max_row_done, 2 * b + 2, 2 * BATCH)
                        MM(misc[:, :], wo_sb[:, :], o_ch[:, :], start=True, stop=True).then_inc(wo_ready, 1)
                    if s == S_QPROJ and exists(b + 2):
                        if is_at(b, -2):
                            pe.wait_ge(small_loaded, 16 * 12)
                        wait(pe, xn_done, b + 3)
                        wait(pe, attn_done, b)
                        wait(pe, max_row_done, 2 * b + 2, 2 * BATCH)
                        MM(misc[:, :], wq_sb[:, :], xin[e][:, :], start=True, stop=True).then_inc(q_ready, 1)
                    if s == S_KPROJ and exists(b + 2):
                        wait(pe, cin_loaded[e], 16 * (p + 2))
                        wait(pe, qb_done, b + 3)
                        MM(misc[:, :], wk_sb[:, :], cin[e][:, :], start=True, stop=True).then_inc(k_ready, 1)
                    if s == S_VPROJ and exists(b + 1):
                        wait(pe, kb_done, b + 3, BATCH)
                        wait(pe, attn_done, b)
                        wait(pe, max_row_done, 2 * b + 2, 2 * BATCH)
                        for j in range(TT):
                            mm = MM(misc[:, P * j:P * j + P], cin[1 - e][:, P * j:P * j + P], wv_sb[:, :],
                                    start=True, stop=True)
                        mm.then_inc(v_ready, 1)
                    if e == 0 and s in (S_XT0, S_XT1) and exists(p - 1, PAIRS):
                        i = 0 if s == S_XT0 else 1
                        wait(pe, xlo_done, 2 * (p - 1) + i + 1)
                        wait(pe, v_done, b + 2, BATCH)
                        wait(pe, attn_done, b)
                        if i:
                            wait(pe, xT_done, 2 * (p - 1) + 1)
                        for k in range(TT):
                            for hl in range(2):
                                c = P * (2 * k + hl)
                                mm = TR(misc16[:, c:c + P], x_hl[i][:, hl, P * k:P * k + P], ident16[:, :])
                        mm.then_inc(xT_ready, 1)
                    if s == 28 and (is_at(b, -1) or is_at(b, 0)):
                        weight_sum(b + 1)
                    if s == 4 and is_at(b, 2):
                        weight_sum(2)

            pe.wait_ge(consts_set, 10)
            pe.wait_ge(ident_set, 4)
            pairs(pe, iteration)

        @block.scalar
        def _(act):
            act.dma_start(stage_a.rearrange("p (t e) -> p t e", t=TT), wupT).then_inc(up_loaded, 16)
            act.dma_start(stage_b.rearrange("p (t e) -> p t e", t=TT), wgateT).then_inc(gate_loaded, 16)
            act.wait_ge(small_loaded, 16 * 12)
            nc.scalar.activation(tgate[:, :], gates[:, :], ACT.Tanh).then_inc(gate_tanh, 1)

            def abs_rows(m, c):
                stage, scratch = [(stage_a, w_up), (stage_b, w_gate), (stage_a, w_down)][m]
                act.wait_ge(w_loaded[m], 16)
                if m == 2:
                    act.wait_ge(quant_done, 16)
                    dst = w_down[:, 4 * c:4 * c + 4, :]
                else:
                    dst = scratch[:, c, :]
                nc.scalar.activation(dst, stage[:, 2048 * c:2048 * c + 2048] if m < 2 else
                                     stage[:, 2048 * c:2048 * c + 2048].rearrange("p (t d) -> p t d", t=4),
                                     ACT.Abs, accum_out=asum[:, m, c:c + 1]).then_inc(abs_done, 1)

            def iteration(p, e):
                b = PAIR * p + e
                for s in range(TILES):
                    S = TILES * e + s
                    if exists(b):
                        wait(act, st_ready, TILES * b + s + 1)
                        if s % 4 == 0:
                            wait(act, pv_done, QUADS * b + s // 4 - 1)
                        nc.scalar.activation(probs[:, s % 8, :], st_ps[s % 2][:, :], ACT.Exp,
                                             scale=1.0 / (SHIFT * float(HD) ** 0.5)).then_inc(exp_done, 1)
                    if (s == 2 and exists(b - 1)) or (s == 18 and exists(b)):
                        ob, g = (b - 1, 1) if s == 2 else (b, 0)
                        wait(act, pv_done, QUADS * ob + 4 * g + 4)
                        wait(act, oT_ready, 2 * (ob - 1) + g + 1)
                        nc.scalar.activation(o_raw[:, g, :], pv_ps[:, :], ACT.Copy).then_inc(o_copied, 1)
                    if s == S_OBACK + 1 and exists(b - 1):
                        wait(act, ob_ready, b)
                        wait(act, wo_ready, b - 1)
                        nc.scalar.activation(o_ch[:, :], misc[:, :], ACT.Copy).then_inc(o_ch_done, 1)
                    if s == S_WO + 1 and exists(b - 1):
                        wait(act, wo_ready, b)
                        wait(act, x1_done, b - 1)
                        nc.scalar.activation(attn[:, :], misc[:, :], ACT.Identity, bias=tbo[:, :],
                                             scale=tgate[:, 0:1]).then_inc(attn_done, 1)
                    if s == S_QPROJ + 1 and exists(b + 2):
                        wait(act, q_ready, b + 3)
                        wait(act, qlo_done, b + 2)
                        if is_at(b, -2):
                            act.wait_ge(dve_small, 1)
                        nc.scalar.activation(qb[:, :], misc[:, :], ACT.Identity, bias=bq16[:, :],
                                             scale=QK_SCALE).then_inc(qb_done, 1)
                    if s == S_KPROJ + 1 and exists(b + 2):
                        wait(act, k_ready, b + 3)
                        wait(act, klo_done, b + 2)
                        nc.scalar.activation(kb[:, :], misc[:, :], ACT.Identity, bias=bk16[:, :],
                                             scale=QK_SCALE).then_inc(kb_done, 1)
                    t = ffn_tile_at(S - 1)
                    if t is not None and exists(p - 1, PAIRS):
                        wait(act, ug_ready, ET * (p - 1) + t + 1)
                        wait(act, hu_done, ET * (p - 1) + t - 1)
                        nc.scalar.activation(th[:, t % 2, :], ff_ps[t % 2][:, 0:256], ACT.Tanh,
                                             scale=up_half[:, :]).then_inc(tanh_done, 1)
                    if s >= 20 and s % 2 == 0 and s < 28 and is_at(b, -1):
                        abs_rows(0, (s - 20) // 2)
                    if s >= 16 and s % 2 == 0 and s < 24 and is_at(b, 0):
                        abs_rows(1, (s - 16) // 2)
                    if s == 28 and is_at(b, 0):
                        act.wait_ge(quant_done, 8)
                        act.dma_start(stage_a.rearrange("p (t d) -> p t d", t=ET), wdownT).then_inc(down_loaded, 16)
                    if s >= 28 and is_at(b, 1):
                        abs_rows(2, s - 28)

            pairs(act, iteration)

        @block.vector
        def _(dve):
            V = nc.vector
            dve.wait_ge(small_loaded, 16 * 12)
            V.tensor_scalar(bq16[:, :], biases[:, 0:1], QK_SCALE, None, ALU.mult)
            V.tensor_scalar(bk16[:, :], biases[:, 1:2], QK_SCALE, None, ALU.mult).then_inc(dve_small, 1)
            dve.wait_ge(gate_tanh, 1)
            V.tensor_scalar(tbo[:, :], biases[:, 2:3], tgate[:, 0:1], None, ALU.mult).then_inc(dve_small, 1)

            def weight_scale(m):
                dve.wait_ge(wsum_ready, m + 1)
                V.reduce_sum(wsum[:, m:m + 1], ff_ps[0][:, 0:4], axis=AX.X).then_inc(wscale_done, 1)
                dve.wait_ge(wscale_done, m + 1)
                V.tensor_scalar(wscale[:, m:m + 1], wsum[:, m:m + 1], 1.0 / (EXPERT * SEQ), TERNARY_EPS,
                                ALU.mult, ALU.add).then_inc(dve_small, 1)
                dve.wait_ge(dve_small, 2 + 2 * m + 1)
                V.tensor_scalar(thr[:, m:m + 1], wscale[:, m:m + 1], 0.5, None, ALU.mult)
                V.tensor_scalar(nthr[:, m:m + 1], wscale[:, m:m + 1], -0.5, None, ALU.mult).then_inc(dve_small, 1)
                dve.wait_ge(dve_small, 2 + 2 * m + 2)

            def quantise(m, c):
                src = [stage_a, stage_b, stage_a][m][:, 1024 * c:1024 * c + 1024]
                if m < 2:
                    dst = [w_up, w_gate][m][:, c // 2, 1024 * (c % 2):1024 * (c % 2) + 1024]
                else:
                    dst = w_down[:, 2 * c:2 * c + 2, :]
                    src = src.rearrange("p (t d) -> p t d", t=2)
                V.tensor_scalar(dst, src, nthr[:, m:m + 1], None, ALU.is_lt).then_inc(quant_low, 1)
                dve.wait_ge(quant_low, 8 * m + c + 1)
                V.scalar_tensor_tensor(out=dst, in0=src, scalar=thr[:, m:m + 1], in1=dst, op0=ALU.is_gt,
                                       op1=ALU.subtract).then_inc(quant_done, 1)

            def ffn_constants():
                V.tensor_scalar(up_half[:, :], wscale[:, 0:1], 0.5 / XN_SCALE, None, ALU.mult)
                V.tensor_tensor(yc1[:, :], wscale[:, 0:1], wscale[:, 1:2], ALU.mult).then_inc(dve_small, 1)
                dve.wait_ge(dve_small, 9)
                V.tensor_tensor(yc2[:, :], yc1[:, :], wscale[:, 2:3], ALU.mult).then_inc(dve_small, 1)
                dve.wait_ge(dve_small, 10)
                V.tensor_scalar(y_coef[:, :], yc2[:, :], tgate[:, 1:2], 0.5 * HID_SCALE, ALU.mult,
                                ALU.mult).then_inc(dve_small, 1)
                dve.wait_ge(dve_small, 11)

            swap = [(i + HD // 2) % HD + HD * (i // HD) for i in range(32)]

            def iteration(p, e):
                b = PAIR * p + e
                for s in range(TILES):
                    S = TILES * e + s
                    mb, m = (b, s + TILES - LAG) if s < LAG else (b + 1, s - LAG)
                    if exists(mb):
                        wait(dve, mx_ready, TILES * mb + m + 1)
                        if m == 0:
                            wait(dve, max16_done, 2 * mb)
                        V.reduce_max(maxima[:, m:m + 1], mx_ps[m % 2][:, :], axis=AX.X).then_inc(mx_done, 1)
                    if (s == LAG - 1 and exists(b)) or (s == LAG + 15 and exists(b + 1)):
                        rb, half = (b, 1) if s == LAG - 1 else (b + 1, 0)
                        wait(dve, mx_done, TILES * rb + 16 * half + 16)
                        wait(dve, maxT_ready, 2 * rb + half - 1)
                        V.tensor_scalar(max16[:, 16 * half:16 * half + 16], maxima[:, 16 * half:16 * half + 16],
                                        1.0 / SHIFT, None, ALU.mult).then_inc(max16_done, 1)
                    if (s == S_ROW1 + 1 and exists(b)) or (s == S_ROW0 + 1 and exists(b + 1)):
                        rb, half = (b, 1) if s == S_ROW1 + 1 else (b + 1, 0)
                        wait(dve, maxT_ready, 2 * rb + half + 1)
                        wait(dve, row_loaded[half], 16 * rb)
                        V.tensor_copy(max_row[half][:, :], misc16[0:16, 0:P]).then_inc(max_row_done, 1)
                    if s == 1 and exists(b + 2):
                        wait(dve, xin_loaded[e], 16 * (p + 2))
                        wait(dve, ve1_done, b + 2)
                        V.bn_stats(stats1[:, :], xin[e][:, :]).then_inc(bn1_done, 1)
                        wait(dve, bn1_done, b + 3)
                        carry_wait(dve)
                        V.bn_aggr(mv1[:, :], stats1[:, :]).then_inc(mv1_done, 1)
                    if s == 4 and exists(b + 2):
                        wait(dve, rstd1_done, b + 3)
                        V.tensor_scalar(xin[e][:, :], xin[e][:, :], mv1[:, 0:1], rstd1[:, :], ALU.subtract,
                                        ALU.mult).then_inc(xn_done, 1)
                    if (s == S_OT1 + 1 and exists(b - 1)) or (s == S_OT0 + 1 and exists(b)):
                        ob, g = (b - 1, 1) if s == S_OT1 + 1 else (b, 0)
                        wait(dve, oT_ready, 2 * ob + g + 1)
                        wait(dve, o_tok_done, 2 * (ob - 1) + g + 1)
                        V.reciprocal(rec[:, g, :], misc[:, HD::2 * HD]).then_inc(rec_done, 1)
                        wait(dve, rec_done, 2 * ob + g + 1)
                        wait(dve, ob_ready, ob)
                        sums = misc[:, :].rearrange("p (t j c) -> p t j c", t=TT, c=2 * HD)[:, :, :, 0:HD]
                        V.tensor_tensor(o_tok[:, :, 64 * g:64 * g + 64].rearrange("p t (j c) -> p t j c", c=HD), sums,
                                        rec[:, g, :].rearrange("p (t j) -> p t j", t=TT).unsqueeze(3)
                                        .to_broadcast([P, TT, GROUP, HD]), ALU.mult).then_inc(o_tok_done, 1)
                    if s == S_WO + 2 and exists(b - 1):
                        wait(dve, attn_done, b)
                        wait(dve, xres_loaded[1 - e], 16 * (p + 1 if e else p))
                        wait(dve, x1_moved, 16 * (p if e else p - 1), 16 * PAIRS)
                        V.tensor_tensor(x1[:, 1 - e, :], attn[:, :], xres[1 - e][:, :], ALU.add).then_inc(x1_done, 1)
                        wait(dve, x1_done, b)
                        wait(dve, rstd2_step, 3 * (b - 1))
                        V.bn_stats(stats2[:, :], x1[:, 1 - e, :]).then_inc(bn2_done, 1)
                        wait(dve, bn2_done, b)
                        carry_wait(dve)
                        V.bn_aggr(mv2[:, :], stats2[:, :]).then_inc(mv2_done, 1)
                    if s == S_WO + 4 and exists(b - 1):
                        wait(dve, rstd2_step, 3 * b)
                        wait(dve, xlo_done, b - 1)
                        V.tensor_scalar(xn2[:, :], x1[:, 1 - e, :], mv2[:, 0:1], rstd2s[:, :], ALU.subtract,
                                        ALU.mult).then_inc(xn2_done, 1)
                        wait(dve, xn2_done, b)
                        wait(dve, xT_ready, b - 2)
                        V.tensor_copy(x_hl[1 - e][:, 0, :], xn2[:, :]).then_inc(xhi_done, 1)
                    if s == S_QPROJ + 2 and exists(b + 2):
                        wait(dve, qb_done, b + 3)
                        wait(dve, rope_q, 3 * (b + 2))
                        carry_wait(dve)
                        V.stream_shuffle(rq[:, :], qb[:, :], swap).then_inc(rq_done, 1)
                    if s == S_KPROJ + 2 and exists(b + 2):
                        wait(dve, kb_done, b + 3)
                        wait(dve, rope_k, 3 * (b + 2))
                        carry_wait(dve)
                        V.stream_shuffle(rk[:, :], kb[:, :], swap).then_inc(rk_done, 1)
                    if s == S_VPROJ + 1 and exists(b + 1):
                        wait(dve, v_ready, b + 2)
                        wait(dve, pv_done, QUADS * b)
                        if is_at(b, -1):
                            dve.wait_ge(consts_set, 10)
                        V.tensor_tensor(v_sb[1 - e][:, :, :, 0:HD],
                                        misc[:, :].rearrange("p (t h c) -> p t h c", t=TT, c=HD),
                                        bv_sb[:, :].rearrange("p (h c) -> p h c", c=HD).unsqueeze(1)
                                        .to_broadcast([P, TT, HEADS, HD]), ALU.add).then_inc(v_done, 1)
                    if s == 18 and exists(b + 2):
                        wait(dve, rope_q, 3 * (b + 3))
                        wait(dve, scr_written, 32 * (b + 2))
                        V.tensor_copy(q_hl[:, 0, :], qb[:, :]).then_inc(qhi_done, 1)
                    if s == 21 and exists(b + 2):
                        wait(dve, rope_k, 3 * (b + 3))
                        V.tensor_copy(k_hl[:, 0, :], kb[:, :]).then_inc(khi_done, 1)
                    if e == 0 and s in (S_XT0 + 1, S_XT1 + 1) and exists(p - 1, PAIRS):
                        i = 0 if s == S_XT0 + 1 else 1
                        wait(dve, xT_ready, 2 * (p - 1) + i + 1)
                        wait(dve, ug_ready, ET * (p - 1))
                        if is_at(p, 1):
                            dve.wait_ge(quant_done, 24)
                        V.tensor_copy(xT[:, :, :, P * i:P * i + P],
                                      misc16.rearrange("p (t l r) -> p t l r", t=TT, l=2)).then_inc(xT_done, 1)
                    t = ffn_tile_at(S - 1)
                    if t is not None and exists(p - 1, PAIRS):
                        n = ET * (p - 1) + t
                        wait(dve, tanh_done, n + 1)
                        wait(dve, hb_done, n)
                        V.scalar_tensor_tensor(out=hu, in0=th[:, t % 2, :], scalar=1.0,
                                               in1=ff_ps[t % 2][:, 0:256], op0=ALU.add, op1=ALU.mult).then_inc(hu_done, 1)
                        wait(dve, hu_done, n + 1)
                        wait(dve, hlo_done, n - 1)
                        V.scalar_tensor_tensor(out=hb[:, t % 2, :], in0=hu, scalar=1.0 / (XN_SCALE * XN_SCALE * HID_SCALE),
                                               in1=ff_ps[t % 2][:, 256:512], op0=ALU.mult, op1=ALU.mult).then_inc(hb_done, 1)
                        wait(dve, hb_done, n + 1)
                        if t == 0:
                            wait(dve, y_ready, 2 * (p - 1))
                        V.tensor_copy(hid[:, t, 0, :], hb[:, t % 2, :]).then_inc(hhi_done, 1)
                    if e == 0 and s in (9, 17) and exists(p - 2, PAIRS):
                        i = 0 if s == 9 else 1
                        wait(dve, y_ready, 2 * (p - 2) + i + 1)
                        wait(dve, x1_moved, 16 * (p - 1))
                        wait(dve, out_written[i], 16 * (p - 1))
                        V.scalar_tensor_tensor(out=y_out[:, i, :], in0=ff_ps[i][:, :], scalar=y_coef[:, :],
                                               in1=x1_res[:, i, :], op0=ALU.mult, op1=ALU.add).then_inc(y_done, 1)
                    if is_at(b, 0):
                        if s == 5:
                            weight_scale(0)
                        if s >= 8 and s % 3 == 2:
                            quantise(0, (s - 8) // 3)
                    if is_at(b, 1):
                        if s == 0:
                            weight_scale(1)
                        if s >= 2 and s % 3 == 2 and s < 26:
                            quantise(1, (s - 2) // 3)
                    if is_at(b, 2):
                        if s == 5:
                            weight_scale(2)
                            ffn_constants()
                        if 6 <= s < 14:
                            quantise(2, s - 6)

            pairs(dve, iteration)

        @block.gpsimd
        def _(pool):
            G = nc.gpsimd
            G.memset(ident[:, :], 0.0).then_inc(ident_set, 1)
            G.memset(ident16[:, :], 0.0).then_inc(ident_set, 1)
            pool.wait_ge(ident_set, 2)
            for t in (ident, ident16):
                G.affine_select(out=t[:, :], in_=t[:, :], compare_op=ALU.not_equal, fill=1.0, base=0,
                                pattern=[[-1, P]], channel_multiplier=1).then_inc(ident_set, 1)
            G.memset(half_neg[:, :], -0.5).then_inc(consts_set, 1)
            for i in range(2):
                G.memset(v_sb[i][:, :, :, HD:2 * HD], 1.0).then_inc(consts_set, 1)
            G.memset(ones[:, :], 1.0).then_inc(consts_set, 1)
            n = 4
            for i in range(2):
                for t in (q_st[i], k_st[i]):
                    pool.wait_ge(consts_set, n)
                    G.memset(t[64:128, :, :], 0.0).then_inc(consts_set, 1)
                    n += 1
            for i in range(2):
                pool.wait_ge(consts_set, n)
                G.memset(k_st[i][SHIFT_ROW:SHIFT_ROW + 1, :, :], -SHIFT).then_inc(consts_set, 1)
                n += 1
            pool.wait_ge(consts_set, n)

            def iteration(p, e):
                b = PAIR * p + e
                for s in range(TILES):
                    S = TILES * e + s
                    if s == 1 and exists(b + 2):
                        wait(pool, mv1_done, b + 3)
                        wait(pool, rstd1_done, b + 2)
                        if is_at(b, -2):
                            pool.wait_ge(consts_set, 10)
                        carry_wait(pool)
                        G.tensor_scalar(ve1[:, :], mv1[:, 1:2], LN_EPS, None, ALU.add).then_inc(ve1_done, 1)
                        wait(pool, ve1_done, b + 3)
                        wait(pool, xn_done, b + 2)
                        G.tensor_tensor(rstd1[:, :], ve1[:, :], half_neg[:, :], ALU.pow).then_inc(rstd1_done, 1)
                    if s == S_WO + 3 and exists(b - 1):
                        wait(pool, mv2_done, b)
                        carry_wait(pool)
                        G.tensor_scalar(ve2[:, :], mv2[:, 1:2], LN_EPS, None, ALU.add).then_inc(rstd2_step, 1)
                        wait(pool, rstd2_step, 3 * (b - 1) + 1)
                        G.tensor_tensor(rstd2[:, :], ve2[:, :], half_neg[:, :], ALU.pow).then_inc(rstd2_step, 1)
                        wait(pool, rstd2_step, 3 * (b - 1) + 2)
                        wait(pool, xn2_done, b - 1)
                        carry_wait(pool)
                        G.tensor_scalar(rstd2s[:, :], rstd2[:, :], XN_SCALE, None, ALU.mult).then_inc(rstd2_step, 1)
                    if s == S_WO + 5 and exists(b - 1):
                        wait(pool, xhi_done, b)
                        G.tensor_tensor(x_hl[1 - e][:, 1, :], xn2[:, :], x_hl[1 - e][:, 0, :],
                                        ALU.subtract).then_inc(xlo_done, 1)
                    for s0, src, turned, turned_done, steps in ((15, qb, rq, rq_done, rope_q), (18, kb, rk, rk_done, rope_k)):
                        if s == s0 and exists(b + 2):
                            wait(pool, turned_done, b + 3)
                            if is_at(b, -2):
                                pool.wait_ge(small_loaded, 16 * 12)
                            G.tensor_tensor(src[:, :], src[:, :], cos_sb[:, :], ALU.mult).then_inc(steps, 1)
                        if s == s0 + 1 and exists(b + 2):
                            G.tensor_tensor(turned[:, :], turned[:, :], sin_sb[:, :], ALU.mult).then_inc(steps, 1)
                        if s == s0 + 2 and exists(b + 2):
                            wait(pool, steps, 3 * (b + 2) + 2)
                            G.tensor_tensor(src[:, :], src[:, :], turned[:, :], ALU.add).then_inc(steps, 1)
                    if s == 21 and exists(b + 2):
                        wait(pool, qhi_done, b + 3)
                        G.tensor_tensor(q_hl[:, 1, :], qb[:, :], q_hl[:, 0, :], ALU.subtract).then_inc(qlo_done, 1)
                    if s == 22 and exists(b + 2):
                        wait(pool, khi_done, b + 3)
                        G.tensor_tensor(k_hl[:, 1, :], kb[:, :], k_hl[:, 0, :], ALU.subtract).then_inc(klo_done, 1)
                    t = ffn_tile_at(S - 1)
                    if t is not None and exists(p - 1, PAIRS):
                        wait(pool, hhi_done, ET * (p - 1) + t + 1)
                        G.tensor_tensor(hid[:, t, 1, :], hb[:, t % 2, :], hid[:, t, 0, :],
                                        ALU.subtract).then_inc(hlo_done, 1)

            pairs(pool, iteration)

        @block.sync
        def _(sp):
            def wait(eng, s, value, total=None):
                if isinstance(value, int):
                    if total is not None:
                        value = min(value, total)
                    if value <= 0:
                        return
                eng.wait_ge(s, value)
                if not isinstance(value, int):
                    carry_wait(eng)

            def row(t, b):
                if isinstance(b, int):
                    return t[b, :, :]
                return t[bass.ds(sp.snap(b), 1), :, :].rearrange("a c t -> (a c) t")

            sp.dma_start(xin[0][:, :], x[0, :, :]).then_inc(xin_loaded[0], 16)
            for i in range(PAIR):
                sp.sem_inc(out_written[i], 16)
            column = lambda v: v.rearrange("(c a) -> c a", a=1)
            for dst, src in ((wq_sb[:, :], wqT), (wk_sb[:, :], wkT), (wv_sb[:, :], wvT), (wo_sb[:, :], woT),
                             (biases[:, 0:1], column(bq)), (biases[:, 1:2], column(bk)), (biases[:, 2:3], column(bo)),
                             (gates[:, 0:1], g_xattn.partition_broadcast(P)), (gates[:, 1:2], g_ffn.partition_broadcast(P)),
                             (bv_sb[:, :], bv.partition_broadcast(P)), (cos_sb[:, :], cos), (sin_sb[:, :], sin)):
                sp.dma_start(dst, src).then_inc(small_loaded, 16)
            sp.dma_start(cin[0][:, :], ctxt[0, :, :]).then_inc(cin_loaded[0], 16)

            def iteration(p, e):
                b = PAIR * p + e
                x_now = row(x, b) if exists(b) else None
                x_next, c_next = (row(x, b + 3), row(ctxt, b + 3)) if exists(b + 3) else (None, None)
                outs = [row(out, PAIR * (p - 2) + i) for i in range(PAIR)] if e == 0 and exists(p - 2, PAIRS) else None
                if exists(b):
                    wait(sp, x1_done, b - 1)
                    sp.dma_start(xres[e][:, :], x_now).then_inc(xres_loaded[e], 16)
                if exists(b + 3):
                    wait(sp, q_ready, b + 2)
                    sp.dma_start(xin[1 - e][:, :], x_next).then_inc(xin_loaded[1 - e], 16)
                if e == 0 and exists(p - 2, PAIRS):
                    wait(sp, y_done, 2 * (p - 2) + 1)
                    sp.dma_start(outs[0], y_out[:, 0, :]).then_inc(out_written[0], 16)
                if exists(b):
                    wait(sp, max_row_done, 2 * b + 2)
                    wait(sp, st_ready, TILES * (b - 1))
                    sp.dma_start(q_st[e][SHIFT_ROW:SHIFT_ROW + 1, GROUP:HEADS, :].rearrange("p h (a t) -> p (h a) t", a=TT),
                                 max_row[1][:, :]).then_inc(row_loaded[1], 16)
                if e == 0 and exists(p - 2, PAIRS):
                    wait(sp, y_done, 2 * (p - 2) + 2)
                    sp.dma_start(outs[1], y_out[:, 1, :]).then_inc(out_written[1], 16)
                if exists(b + 3):
                    wait(sp, v_ready, b + 2)
                    sp.dma_start(cin[1 - e][:, :], c_next).then_inc(cin_loaded[1 - e], 16)
                if e == 0 and exists(p - 1, PAIRS):
                    wait(sp, x1_done, 2 * p)
                    wait(sp, y_done, 2 * (p - 1))
                    if is_at(p, 1):
                        sp.wait_ge(quant_done, 24)
                    sp.dma_start(x1_res, x1[:, :, :]).then_inc(x1_moved, 16)
                if exists(b + 1):
                    wait(sp, max_row_done, 2 * (b + 1) + 1)
                    sp.dma_start(q_st[1 - e][SHIFT_ROW:SHIFT_ROW + 1, 0:GROUP, :].rearrange("p h (a t) -> p (h a) t", a=TT),
                                 max_row[0][:, :]).then_inc(row_loaded[0], 16)
                if exists(b + 2):
                    wait(sp, st_loaded[1 - e], 128 * (p + 2 if e else p + 1))
                    wait(sp, qlo_done, b + 3)
                    sp.dma_start(q_scr.rearrange("l p t -> p l t"), q_hl[:, :, :]).then_inc(scr_written, 16)
                    wait(sp, klo_done, b + 3)
                    sp.dma_start(k_scr.rearrange("l p t -> p l t"), k_hl[:, :, :]).then_inc(scr_written, 16)
                    wait(sp, st_ready, TILES * (b + 1))
                    wait(sp, scr_written, 32 * (b + 3))
                    for l in range(2):
                        for r in range(2):
                            qr, kr = 32 * r + 16 * l, 32 * l + 16 * r
                            sp.dma_start(q_st[e][qr:qr + HD, :, :],
                                         q_scr[l, :, :].rearrange("(h c) t -> c h t", c=HD)).then_inc(st_loaded[e], 16)
                            sp.dma_start(k_st[e][kr:kr + HD, :, :],
                                         k_scr[l, :, :].rearrange("(h c) t -> c h t", c=HD)).then_inc(st_loaded[e], 16)

            pairs(sp, iteration, last=PAIRS - 3)
            for i in range(PAIR):
                sp.wait_ge(out_written[i], 16 * (PAIRS + 1))


def _tables():
    inv = (np.float32(1.0) / np.float32(10000.0) ** (np.arange(0, HD, 2, dtype=np.float32) / np.float32(HD))).astype(np.float32)
    f = np.arange(SEQ, dtype=np.float32)[:, None] * inv[None, :]
    f = np.concatenate([f, f], axis=-1).astype(np.float32)
    sign = np.where(np.arange(HD) < HD // 2, np.float32(-1.0), np.float32(1.0))
    cos = np.tile(np.cos(f).T, (HEADS, 1)).astype(np.float32)
    sin = np.tile((np.sin(f) * sign[None, :]).T, (HEADS, 1)).astype(np.float32)
    return np.ascontiguousarray(cos), np.ascontiguousarray(sin)


def kernel(x, ctx_2048, g_xattn, g_ffn, L0_xattn_Wq, L0_xattn_bq, L0_xattn_Wk, L0_xattn_bk, L0_xattn_Wv,
           L0_xattn_bv, L0_xattn_Wo, L0_xattn_bo, L0_ffn_W_up, L0_ffn_W_gate, L0_ffn_W_down):
    import concourse.bacc as _bacc
    from concourse.bass_utils import run_bass_kernel_spmd as _run

    a = np.asarray

    def tiles(w):
        w = a(w).T
        return np.ascontiguousarray(w.reshape(w.shape[0] // P, P, w.shape[1]).transpose(1, 0, 2))

    cos, sin = _tables()
    ins = {
        "x": a(x), "ctxt": a(ctx_2048), "g_xattn": a(g_xattn), "g_ffn": a(g_ffn),
        "wqT": a(L0_xattn_Wq).T, "bq": a(L0_xattn_bq), "wkT": a(L0_xattn_Wk).T, "bk": a(L0_xattn_bk),
        "wvT": a(L0_xattn_Wv).T, "bv": a(L0_xattn_bv), "woT": a(L0_xattn_Wo).T, "bo": a(L0_xattn_bo),
        "wupT": tiles(L0_ffn_W_up), "wgateT": tiles(L0_ffn_W_gate), "wdownT": tiles(L0_ffn_W_down),
        "cos": cos, "sin": sin,
    }
    nc = _bacc.Bacc("TRN2", target_bir_lowering=False, num_devices=1)
    arrays, args = {}, []
    for name, v in ins.items():
        v = np.ascontiguousarray(v)
        arrays[f"in_{name}"] = v
        args.append(nc.dram_tensor(f"in_{name}", v.shape, mybir.dt.from_np(v.dtype), kind="ExternalInput").ap())
    out = nc.dram_tensor("out_0", (BATCH, CH, SEQ), mybir.dt.float32, kind="ExternalOutput").ap()
    flamingo_block(nc, *args, out)
    r = _run(nc, [arrays], core_ids=[0])
    return r.results[0]["out_0"]
```

```python
import numpy as np
import concourse.bass as bass
from concourse import mybir
from contextlib import ExitStack

BATCH, CH, SEQ = 16, 128, 512
HEADS = 8
HD = CH // HEADS
EXPERT = 2048
P = 128
TT = SEQ // P
ET = EXPERT // P
GROUP = HEADS // 2
PAIR = 2
PAIRS = BATCH // PAIR
TILES = HEADS * TT
QUADS = TILES // GROUP
QK_SCALE = 16.0
SHIFT = QK_SCALE * QK_SCALE
XN_SCALE = 2048.0
HID_SCALE = 16.0
LAG = 6
SMALL = 5 * CH + 5
MAGIC = 1.5 * 2.0 ** 23
SHIFT_ROW = 96
LN_EPS = 1e-5
TERNARY_EPS = 1e-8

S_OT1, S_OBACK, S_WO, S_ROW1 = 3, 5, 7, 8
S_QPROJ, S_KPROJ, S_VPROJ, S_XT0, S_XT1, S_OT0, S_ROW0 = 11, 13, 15, 17, 19, 22, 25
W_ABS_AT = ((-2, 16), (-1, 17), (0, 28))
W_SUM_AT = ((-2, 21), (-1, 21), (1, 1))
W_SCALE_AT = ((-2, 22), (-1, 22), (1, 2))
W_ROUND_AT = ((-2, 24), (-1, 24), (1, 4))
W_QUANT_AT = ((-1, 6), (0, 8), (1, 16))
S_DOWN = 2
S_FFN = 22


def flamingo_block(nc, x, ctxt, attn_weights, rotary, wupT, wgateT, wdownT, out):
    f32, f16 = mybir.dt.float32, mybir.dt.float16
    ALU, ACT, AX = mybir.AluOpType, mybir.ActivationFunctionType, mybir.AxisListType

    ctx = ExitStack()
    with ctx:
        def sb(name, shape, dt=f32):
            return ctx.enter_context(nc.sbuf_tensor(name, shape, dt))

        def sem(name):
            return ctx.enter_context(nc.semaphore(name))

        arena = sb("arena", [P, 16384])
        stage_a = arena[:, 0:8192]
        stage_b = arena[:, 8192:16384]
        w_up = sb("w_up", [P, TT, EXPERT], f16)
        w_gate = sb("w_gate", [P, TT, EXPERT], f16)
        w_down = arena[:, 12288:16384].bitcast(f16).rearrange("p (t d) -> p t d", t=ET)
        hid = arena[:, 0:4096].bitcast(f16).rearrange("p (e l r) -> p e l r", e=ET, l=2)
        x1_res = arena[:, 4096:5120].rearrange("p (b t) -> p b t", b=PAIR)
        y_out = arena[:, 5120:6144].rearrange("p (b t) -> p b t", b=PAIR)
        xT = arena[:, 6144:7168].bitcast(f16).rearrange("p (t l r) -> p t l r", t=TT, l=2)
        th = arena[:, 7168:7680].rearrange("p (b r) -> p b r", b=2)
        hu = arena[:, 7680:7936]
        hb = arena[:, 7936:8448].rearrange("p (b r) -> p b r", b=2)

        q_st = [sb(f"q_st{i}", [P, HEADS, SEQ], f16) for i in range(2)]
        k_st = [sb(f"k_st{i}", [P, HEADS, SEQ], f16) for i in range(2)]
        probs = sb("probs", [P, 2 * GROUP, SEQ])
        xin = [sb(f"xin{i}", [P, SEQ]) for i in range(2)]
        cin = [sb(f"cin{i}", [P, SEQ]) for i in range(2)]
        xres = [sb(f"xres{i}", [P, SEQ]) for i in range(2)]
        tables = sb("tables", [P, 2, SEQ])
        cos_sb, sin_sb = tables[:, 0, :], tables[:, 1, :]
        qb, kb, rq, rk = (sb(n, [P, SEQ]) for n in ("qb", "kb", "rq", "rk"))
        q_hl, k_hl = sb("q_hl", [P, 2, SEQ], f16), sb("k_hl", [P, 2, SEQ], f16)
        v_sb = [sb(f"v_sb{i}", [P, TT, HEADS, 2 * HD]) for i in range(2)]
        o_raw = sb("o_raw", [P, 2, SEQ])
        o_tok = sb("o_tok", [P, TT, CH])
        o_ch = sb("o_ch", [P, SEQ])
        attn = sb("attn", [P, SEQ])
        x1 = sb("x1", [P, PAIR, SEQ])
        xn2 = sb("xn2", [P, SEQ])
        x_hl = [sb(f"x_hl{i}", [P, 2, SEQ], f16) for i in range(2)]
        small = sb("small", [P, SMALL])
        wq_sb, wk_sb, wv_sb, wo_sb, bv_sb = (small[:, CH * i:CH * (i + 1)] for i in range(5))
        biases = small[:, 5 * CH:5 * CH + 3]
        gates = small[:, 5 * CH + 3:5 * CH + 5]
        ident = sb("ident", [P, P])
        ident16 = sb("ident16", [P, P], f16)
        ones = sb("ones", [P, P])
        maxima = sb("maxima", [P, TILES])
        max16 = sb("max16", [P, TILES], f16)
        max_row = [sb(f"max_row{i}", [16, P], f16) for i in range(2)]
        rec = sb("rec", [P, 2, 16])
        stats1, mv1, stats2, mv2 = sb("stats1", [P, 6]), sb("mv1", [P, 2]), sb("stats2", [P, 6]), sb("mv2", [P, 2])
        ve1, rstd1, ve2, rstd2, rstd2s = (sb(n, [P, 1]) for n in ("ve1", "rstd1", "ve2", "rstd2", "rstd2s"))
        half_neg = sb("half_neg", [P, 1])
        tgate = sb("tgate", [P, 2])
        bq16, bk16, tbo = sb("bq16", [P, 1]), sb("bk16", [P, 1]), sb("tbo", [P, 1])
        asum = sb("asum", [P, 3, 4])
        wscale = sb("wscale", [P, 3])
        wsum = sb("wsum", [P, 3])
        winv = sb("winv", [P, 3])
        magic = sb("magic", [P, 1])
        up_half = sb("up_half", [P, 1])
        yc1, yc2, y_coef = sb("yc1", [P, 1]), sb("yc2", [P, 1]), sb("y_coef", [P, 1])

        q_scr = nc.dram_tensor("q_scr", [2, P, SEQ], f16, kind="Internal").ap()
        k_scr = nc.dram_tensor("k_scr", [2, P, SEQ], f16, kind="Internal").ap()

        def bank(name):
            return ctx.enter_context(nc.psum_tensor(name, [P, 512], f32))

        st_ps = [bank("st_ps0"), bank("st_ps1")]
        mx_ps = [bank("mx_ps0"), bank("mx_ps1")]
        pv_ps = bank("pv_ps")
        misc = bank("misc")
        ff_ps = [bank("ff_ps0"), bank("ff_ps1")]
        misc16 = misc[:, :].bitcast(f16)

        consts_set, ident_set = sem("consts_set"), sem("ident_set")
        small_loaded, tables_loaded, dve_small = sem("small_loaded"), sem("tables_loaded"), sem("dve_small")
        rows_zero, v_ones = sem("rows_zero"), sem("v_ones")
        gate_tanh = sem("gate_tanh")
        up_loaded, gate_loaded, down_loaded = ([sem(f"{n}_loaded{c}") for c in range(4)] for n in ("up", "gate", "down"))
        w_loaded = [up_loaded, gate_loaded, down_loaded]
        abs_done, wsum_ready, wscale_done, winv_done = (sem(n) for n in ("abs_done", "wsum_ready", "wscale_done", "winv_done"))
        rounded, clipped_above, quant_done = sem("rounded"), sem("clipped_above"), sem("quant_done")
        xin_loaded = [sem("xin_loaded0"), sem("xin_loaded1")]
        cin_loaded = [sem("cin_loaded0"), sem("cin_loaded1")]
        xres_loaded = [sem("xres_loaded0"), sem("xres_loaded1")]
        bn1_done, mv1_done, ve1_done, rstd1_done, xn_done = (sem(n) for n in ("bn1_done", "mv1_done", "ve1_done", "rstd1_done", "xn_done"))
        q_ready, k_ready, v_ready = sem("q_ready"), sem("k_ready"), sem("v_ready")
        qb_done, kb_done, v_done = sem("qb_done"), sem("kb_done"), sem("v_done")
        rq_done, rk_done = sem("rq_done"), sem("rk_done")
        rope_q, rope_k = sem("rope_q"), sem("rope_k")
        qhi_done, khi_done, qlo_done, klo_done = (sem(n) for n in ("qhi_done", "khi_done", "qlo_done", "klo_done"))
        scr_written = sem("scr_written")
        st_loaded = [sem("st_loaded0"), sem("st_loaded1")]
        mx_ready, mx_done, max16_done, maxT_ready, max_row_done = (sem(n) for n in ("mx_ready", "mx_done", "max16_done", "maxT_ready", "max_row_done"))
        row_loaded = [sem("row_loaded0"), sem("row_loaded1")]
        st_ready, exp_done, pv_done, o_copied = (sem(n) for n in ("st_ready", "exp_done", "pv_done", "o_copied"))
        oT_ready, rec_done, o_tok_done, ob_ready, o_ch_done = (sem(n) for n in ("oT_ready", "rec_done", "o_tok_done", "ob_ready", "o_ch_done"))
        wo_ready, attn_done, x1_done = sem("wo_ready"), sem("attn_done"), sem("x1_done")
        bn2_done, mv2_done, rstd2_step, xn2_done, xhi_done, xlo_done = (sem(n) for n in ("bn2_done", "mv2_done", "rstd2_step", "xn2_done", "xhi_done", "xlo_done"))
        xT_ready, xT_done = sem("xT_ready"), sem("xT_done")
        ug_ready, tanh_done, hu_done, hb_done, hhi_done, hlo_done = (sem(n) for n in ("ug_ready", "tanh_done", "hu_done", "hb_done", "hhi_done", "hlo_done"))
        x1_moved, y_ready, y_done = sem("x1_moved"), sem("y_ready"), sem("y_done")
        out_written = [sem("out_written0"), sem("out_written1")]
        passed = sem("passed")
        block = ctx.enter_context(nc.Block())

        def wait(eng, s, value, total=None):
            if isinstance(value, int):
                if total is not None:
                    value = min(value, total)
                if value <= 0:
                    return
            eng.wait_ge(s, value)

        def carry_wait(eng):
            eng.sem_inc(passed, 1)

        def exists(b, count=BATCH):
            return not isinstance(b, int) or 0 <= b < count

        def is_at(b, n):
            return isinstance(b, int) and b == n

        def pairs(eng, iteration, last=PAIRS - 2):
            for p in (-1, 0, 1):
                for e in range(PAIR):
                    iteration(p, e)
            with eng.Fori(2, last + 1) as p:
                for e in range(PAIR):
                    iteration(p, e)
            for p in range(last + 1, PAIRS + 2):
                for e in range(PAIR):
                    iteration(p, e)

        def up_gate_span(S):
            n = [min(max(16 * ET * k // (2 * TILES - 1 - S_FFN), 0), 16 * ET) for k in (S - S_FFN, S - S_FFN + 1)]
            return range(*n)

        def ffn_tile_at(S):
            done = [n // 16 for n in up_gate_span(S) if n % 16 == 15]
            return done[0] if done else None

        @block.tensor
        def _(pe):
            MM, TR = nc.tensor.matmul, nc.tensor.transpose

            def weight_sum(m):
                pe.wait_ge(consts_set, 2)
                pe.wait_ge(abs_done, 4 * (m + 1))
                if m:
                    pe.wait_ge(wscale_done, m)
                MM(ff_ps[0][:, 0:4], ones[:, :], asum[:, m, :], start=True, stop=True).then_inc(wsum_ready, 1)

            def iteration(p, e):
                b = PAIR * p + e
                for s in range(TILES):
                    S = TILES * e + s
                    if exists(b):
                        if s == 0:
                            wait(pe, row_loaded[0], 16 * (b + 1))
                        if s == TILES // 2:
                            wait(pe, row_loaded[1], 16 * (b + 1))
                        h, j = GROUP * (s // 16) + s % 4, (s % 16) // 4
                        wait(pe, exp_done, TILES * b + s - 1)
                        MM(st_ps[s % 2][:, :], k_st[e][0:SHIFT_ROW + 1, h, P * j:P * j + P], q_st[e][0:SHIFT_ROW + 1, h, :],
                           start=True, stop=True).then_inc(st_ready, 1)
                    mb, m = (b, s + TILES - LAG) if s < LAG else (b + 1, s - LAG)
                    me = e if s < LAG else 1 - e
                    if exists(mb):
                        if m == 0 and (is_at(mb, 0) or is_at(mb, 1)):
                            pe.wait_ge(consts_set, 6)
                            pe.wait_ge(rows_zero, 4)
                        if m == 0:
                            wait(pe, st_loaded[me], 128 * (p + 2 if e else p + 1))
                        h, j = m // TT, m % TT
                        wait(pe, mx_done, TILES * mb + m - 1)
                        MM(mx_ps[m % 2][:, :], q_st[me][0:SHIFT_ROW, h, P * j:P * j + P],
                           k_st[me][0:SHIFT_ROW, h, :], start=True, stop=True).then_inc(mx_ready, 1)
                    if exists(p - 1, PAIRS):
                        for n in up_gate_span(S):
                            t, r = n // 16, n % 16
                            if n == 0:
                                wait(pe, xT_done, 2 * p)
                                if is_at(p, 1):
                                    pe.wait_ge(quant_done, 24)
                            if n == 0:
                                wait(pe, y_done, 2 * (p - 1) - 1)
                            if n == 16:
                                wait(pe, y_done, 2 * (p - 1))
                            if r == 0:
                                wait(pe, hb_done, ET * (p - 1) + t - 1)
                            w, c = (w_up, 0) if r < 8 else (w_gate, 256)
                            k, hl = (r % 8) // 2, r % 2
                            mm = MM(ff_ps[t % 2][:, c:c + 256], w[:, k, P * t:P * t + P], xT[:, k, hl, :],
                                    start=(r % 8 == 0), stop=(r % 8 == 7))
                            if r == 15:
                                mm.then_inc(ug_ready, 1)
                    if exists(p - 2, PAIRS) and S_DOWN <= S < S_DOWN + 16:
                        for n in range(4 * (S - S_DOWN), 4 * (S - S_DOWN) + 4):
                            i, t, hl = n // 32, (n % 32) // 2, n % 2
                            if n % 32 == 0:
                                wait(pe, hb_done, ET * (p - 1) - 1 + i)
                            if i == 0 and hl == 0:
                                wait(pe, hlo_done, ET * (p - 2) + t + 1)
                            mm = MM(ff_ps[i][:, :], hid[:, t, hl, P * i:P * i + P], w_down[:, t, :],
                                    start=(n % 32 == 0), stop=(n % 32 == 31))
                        if n % 32 == 31:
                            mm.then_inc(y_ready, 1)
                    qb_, k = (b, (s - 5) // 4) if s >= 5 else (b - 1, QUADS - 1)
                    if s % 4 == 1 and exists(qb_):
                        ve = e if s >= 5 else 1 - e
                        g, j = k // 4, k % 4
                        wait(pe, exp_done, TILES * qb_ + 4 * k + 4)
                        if k == 0:
                            wait(pe, v_done, qb_ + 1)
                            if is_at(qb_, 0):
                                pe.wait_ge(v_ones, 2)
                        if k % 4 == 0:
                            wait(pe, o_copied, 2 * qb_ + g)
                        for a in range(GROUP):
                            mm = MM(pv_ps[32 * a:32 * a + 32, :], v_sb[ve][:, j, GROUP * g + a, :],
                                    probs[:, (4 * k + a) % 8, :], start=(j == 0), stop=(j == TT - 1))
                        mm.then_inc(pv_done, 1)
                    if (s == S_OT1 and exists(b - 1)) or (s == S_OT0 and exists(b)):
                        ob, g = (b - 1, 1) if s == S_OT1 else (b, 0)
                        wait(pe, o_copied, 2 * ob + g + 1)
                        if g:
                            wait(pe, o_tok_done, 2 * ob + g)
                            wait(pe, max_row_done, 2 * (ob + 1) + 1, 2 * BATCH)
                        else:
                            wait(pe, v_done, b + 2, BATCH)
                            wait(pe, attn_done, b)
                            if e == 0:
                                wait(pe, xT_done, 2 * p)
                        for j in range(TT):
                            mm = TR(misc[:, P * j:P * j + P], o_raw[:, g, P * j:P * j + P], ident[:, :])
                        mm.then_inc(oT_ready, 1)
                    if s == S_OBACK and exists(b - 1):
                        wait(pe, o_tok_done, 2 * b)
                        for j in range(TT):
                            mm = TR(misc[:, P * j:P * j + P], o_tok[:, j, :], ident[:, :])
                        mm.then_inc(ob_ready, 1)
                    if (s == S_ROW1 and exists(b)) or (s == S_ROW0 and exists(b + 1)):
                        rb, half = (b, 1) if s == S_ROW1 else (b + 1, 0)
                        wait(pe, max16_done, 2 * rb + half + 1)
                        if half:
                            wait(pe, attn_done, b)
                            wait(pe, max_row_done, 2 * b + 1)
                        else:
                            wait(pe, o_tok_done, 2 * b + 1)
                            wait(pe, v_done, b + 2, BATCH)
                        TR(misc16[0:16, 0:P], max16[:, 16 * half:16 * half + 16], ident16[:, :]).then_inc(maxT_ready, 1)
                    if s == S_WO and exists(b - 1):
                        wait(pe, o_ch_done, b)
                        MM(misc[:, :], wo_sb, o_ch[:, :], start=True, stop=True).then_inc(wo_ready, 1)
                    if s == S_QPROJ and exists(b + 2):
                        if is_at(b, -2):
                            pe.wait_ge(small_loaded, 16)
                        wait(pe, xn_done, b + 3)
                        wait(pe, attn_done, b)
                        wait(pe, max_row_done, 2 * b + 2, 2 * BATCH)
                        MM(misc[:, :], wq_sb, xin[e][:, :], start=True, stop=True).then_inc(q_ready, 1)
                    if s == S_KPROJ and exists(b + 2):
                        wait(pe, cin_loaded[e], 16 * (p + 2))
                        wait(pe, qb_done, b + 3)
                        MM(misc[:, :], wk_sb, cin[e][:, :], start=True, stop=True).then_inc(k_ready, 1)
                    if s == S_VPROJ and exists(b + 1):
                        wait(pe, kb_done, b + 3, BATCH)
                        wait(pe, attn_done, b)
                        wait(pe, max_row_done, 2 * b + 2, 2 * BATCH)
                        for j in range(TT):
                            mm = MM(misc[:, P * j:P * j + P], cin[1 - e][:, P * j:P * j + P], wv_sb,
                                    start=True, stop=True)
                        mm.then_inc(v_ready, 1)
                    if e == 0 and s in (S_XT0, S_XT1) and exists(p - 1, PAIRS):
                        i = 0 if s == S_XT0 else 1
                        wait(pe, xlo_done, 2 * (p - 1) + i + 1)
                        wait(pe, v_done, b + 2, BATCH)
                        wait(pe, attn_done, b)
                        if i:
                            wait(pe, xT_done, 2 * (p - 1) + 1)
                        for k in range(TT):
                            for hl in range(2):
                                c = P * (2 * k + hl)
                                mm = TR(misc16[:, c:c + P], x_hl[i][:, hl, P * k:P * k + P], ident16[:, :])
                        mm.then_inc(xT_ready, 1)
                    for m, at in enumerate(W_SUM_AT):
                        if isinstance(b, int) and (b, s) == at:
                            weight_sum(m)

            pairs(pe, iteration)

        @block.scalar
        def _(act):
            def load_weights(m, src):
                stage = stage_b if m == 1 else stage_a
                for c in range(4):
                    act.dma_start(stage[:, 2048 * c:2048 * c + 2048], src[:, 2048 * c:2048 * c + 2048]).then_inc(w_loaded[m][c], 16)

            act.wait_ge(small_loaded, 16)
            nc.scalar.activation(tgate[:, :], gates, ACT.Tanh).then_inc(gate_tanh, 1)
            act.wait_ge(cin_loaded[0], 16)
            load_weights(0, wupT)
            load_weights(1, wgateT)

            def quarter(m, c):
                stage = stage_b if m == 1 else stage_a
                return stage[:, 2048 * c:2048 * c + 2048]

            def ternary_quarter(m, c):
                if m == 2:
                    return w_down[:, 4 * c:4 * c + 4, :].rearrange("p t d -> p (t d)")
                return (w_up, w_gate)[m][:, c, :]

            def abs_rows(m, c):
                act.wait_ge(w_loaded[m][c], 16)
                if m == 2:
                    act.wait_ge(quant_done, 16)
                nc.scalar.activation(ternary_quarter(m, c), quarter(m, c), ACT.Abs,
                                     accum_out=asum[:, m, c:c + 1]).then_inc(abs_done, 1)

            def round_quarter(m, c):
                act.wait_ge(winv_done, m + 1)
                act.wait_ge(abs_done, 4 * m + c + 1)
                nc.scalar.activation(quarter(m, c), quarter(m, c), ACT.Identity, bias=magic[:, :],
                                     scale=winv[:, m:m + 1]).then_inc(rounded, 1)

            def iteration(p, e):
                b = PAIR * p + e
                for s in range(TILES):
                    S = TILES * e + s
                    if exists(b):
                        wait(act, st_ready, TILES * b + s + 1)
                        if s % 4 == 0:
                            wait(act, pv_done, QUADS * b + s // 4 - 1)
                        nc.scalar.activation(probs[:, s % 8, :], st_ps[s % 2][:, :], ACT.Exp,
                                             scale=1.0 / (SHIFT * float(HD) ** 0.5)).then_inc(exp_done, 1)
                    if (s == 2 and exists(b - 1)) or (s == 18 and exists(b)):
                        ob, g = (b - 1, 1) if s == 2 else (b, 0)
                        wait(act, pv_done, QUADS * ob + 4 * g + 4)
                        wait(act, oT_ready, 2 * (ob - 1) + g + 1)
                        nc.scalar.activation(o_raw[:, g, :], pv_ps[:, :], ACT.Copy).then_inc(o_copied, 1)
                    if s == S_OBACK + 1 and exists(b - 1):
                        wait(act, ob_ready, b)
                        wait(act, wo_ready, b - 1)
                        nc.scalar.activation(o_ch[:, :], misc[:, :], ACT.Copy).then_inc(o_ch_done, 1)
                    if s == S_WO + 1 and exists(b - 1):
                        wait(act, wo_ready, b)
                        wait(act, x1_done, b - 1)
                        nc.scalar.activation(attn[:, :], misc[:, :], ACT.Identity, bias=tbo[:, :],
                                             scale=tgate[:, 0:1]).then_inc(attn_done, 1)
                    if e == 0 and s in (S_XT0 + 1, S_XT1 + 1) and exists(p - 1, PAIRS):
                        i = 0 if s == S_XT0 + 1 else 1
                        wait(act, xT_ready, 2 * (p - 1) + i + 1)
                        wait(act, ug_ready, ET * (p - 1))
                        if is_at(p, 1):
                            act.wait_ge(quant_done, 24)
                        nc.scalar.activation(xT[:, :, :, P * i:P * i + P],
                                             misc16.rearrange("p (t l r) -> p t l r", t=TT, l=2),
                                             ACT.Copy).then_inc(xT_done, 1)
                    if s == S_QPROJ + 1 and exists(b + 2):
                        wait(act, q_ready, b + 3)
                        wait(act, qlo_done, b + 2)
                        if is_at(b, -2):
                            act.wait_ge(dve_small, 1)
                        nc.scalar.activation(qb[:, :], misc[:, :], ACT.Identity, bias=bq16[:, :],
                                             scale=QK_SCALE).then_inc(qb_done, 1)
                    if s == S_KPROJ + 1 and exists(b + 2):
                        wait(act, k_ready, b + 3)
                        wait(act, klo_done, b + 2)
                        nc.scalar.activation(kb[:, :], misc[:, :], ACT.Identity, bias=bk16[:, :],
                                             scale=QK_SCALE).then_inc(kb_done, 1)
                    t = ffn_tile_at(S - 1)
                    if t is not None and exists(p - 1, PAIRS):
                        wait(act, ug_ready, ET * (p - 1) + t + 1)
                        wait(act, hu_done, ET * (p - 1) + t - 1)
                        nc.scalar.activation(th[:, t % 2, :], ff_ps[t % 2][:, 0:256], ACT.Tanh,
                                             scale=up_half[:, :]).then_inc(tanh_done, 1)
                    for m in range(3):
                        for c in range(4):
                            if not isinstance(b, int):
                                continue
                            if (b, s - c) == W_ABS_AT[m]:
                                abs_rows(m, c)
                            if (b, s - c) == W_ROUND_AT[m]:
                                round_quarter(m, c)
                    if is_at(b, -1) and s == 16:
                        act.wait_ge(quant_done, 8)
                        load_weights(2, wdownT)

            pairs(act, iteration)

        @block.vector
        def _(dve):
            V = nc.vector
            for t in (q_st[0], k_st[0], q_st[1], k_st[1]):
                V.memset(t[64:SHIFT_ROW, :, :].rearrange("p h t -> p (h t)").bitcast(f32), 0.0).then_inc(rows_zero, 1)
            V.memset(magic[:, :], MAGIC)
            dve.wait_ge(small_loaded, 16)
            V.tensor_scalar(bq16[:, :], biases[:, 0:1], QK_SCALE, None, ALU.mult)
            V.tensor_scalar(bk16[:, :], biases[:, 1:2], QK_SCALE, None, ALU.mult).then_inc(dve_small, 1)
            dve.wait_ge(gate_tanh, 1)
            V.tensor_scalar(tbo[:, :], biases[:, 2:3], tgate[:, 0:1], None, ALU.mult).then_inc(dve_small, 1)

            def weight_scale(m):
                dve.wait_ge(wsum_ready, m + 1)
                V.reduce_sum(wsum[:, m:m + 1], ff_ps[0][:, 0:4], axis=AX.X).then_inc(wscale_done, 1)
                dve.wait_ge(wscale_done, m + 1)
                V.tensor_scalar(wscale[:, m:m + 1], wsum[:, m:m + 1], 1.0 / (EXPERT * SEQ), TERNARY_EPS,
                                ALU.mult, ALU.add).then_inc(dve_small, 1)
                dve.wait_ge(dve_small, 2 + m + 1)
                V.reciprocal(winv[:, m:m + 1], wscale[:, m:m + 1]).then_inc(winv_done, 1)

            def quantise(m, c):
                src = [stage_a, stage_b, stage_a][m][:, 1024 * c:1024 * c + 1024]
                if m < 2:
                    dst = [w_up, w_gate][m][:, c // 2, 1024 * (c % 2):1024 * (c % 2) + 1024]
                else:
                    dst = w_down[:, 2 * c:2 * c + 2, :].rearrange("p t d -> p (t d)")
                dve.wait_ge(rounded, 4 * m + c // 2 + 1)
                V.tensor_scalar(dst, src, MAGIC + 1.0, MAGIC, ALU.min, ALU.subtract).then_inc(clipped_above, 1)
                dve.wait_ge(clipped_above, 8 * m + c + 1)
                V.tensor_scalar(dst, dst, -1.0, None, ALU.max).then_inc(quant_done, 1)

            def ffn_constants():
                V.tensor_scalar(up_half[:, :], wscale[:, 0:1], 0.5 / XN_SCALE, None, ALU.mult)
                V.tensor_tensor(yc1[:, :], wscale[:, 0:1], wscale[:, 1:2], ALU.mult).then_inc(dve_small, 1)
                dve.wait_ge(dve_small, 6)
                V.tensor_tensor(yc2[:, :], yc1[:, :], wscale[:, 2:3], ALU.mult).then_inc(dve_small, 1)
                dve.wait_ge(dve_small, 7)
                V.tensor_scalar(y_coef[:, :], yc2[:, :], tgate[:, 1:2], 0.5 * HID_SCALE, ALU.mult,
                                ALU.mult).then_inc(dve_small, 1)
                dve.wait_ge(dve_small, 8)

            swap = [(i + HD // 2) % HD + HD * (i // HD) for i in range(32)]

            def iteration(p, e):
                b = PAIR * p + e
                for s in range(TILES):
                    S = TILES * e + s
                    mb, m = (b, s + TILES - LAG) if s < LAG else (b + 1, s - LAG)
                    if exists(mb):
                        wait(dve, mx_ready, TILES * mb + m + 1)
                        if m == 0:
                            wait(dve, max16_done, 2 * mb)
                        V.reduce_max(maxima[:, m:m + 1], mx_ps[m % 2][:, :], axis=AX.X).then_inc(mx_done, 1)
                    if (s == LAG - 1 and exists(b)) or (s == LAG + 15 and exists(b + 1)):
                        rb, half = (b, 1) if s == LAG - 1 else (b + 1, 0)
                        wait(dve, mx_done, TILES * rb + 16 * half + 16)
                        wait(dve, maxT_ready, 2 * rb + half - 1)
                        V.tensor_scalar(max16[:, 16 * half:16 * half + 16], maxima[:, 16 * half:16 * half + 16],
                                        1.0 / SHIFT, None, ALU.mult).then_inc(max16_done, 1)
                    if (s == S_ROW1 + 1 and exists(b)) or (s == S_ROW0 + 1 and exists(b + 1)):
                        rb, half = (b, 1) if s == S_ROW1 + 1 else (b + 1, 0)
                        wait(dve, maxT_ready, 2 * rb + half + 1)
                        wait(dve, row_loaded[half], 16 * rb)
                        V.tensor_copy(max_row[half][:, :], misc16[0:16, 0:P]).then_inc(max_row_done, 1)
                    if s == 1 and exists(b + 2):
                        wait(dve, xin_loaded[e], 16 * (p + 2))
                        wait(dve, ve1_done, b + 2)
                        V.bn_stats(stats1[:, :], xin[e][:, :]).then_inc(bn1_done, 1)
                        wait(dve, bn1_done, b + 3)
                        carry_wait(dve)
                        V.bn_aggr(mv1[:, :], stats1[:, :]).then_inc(mv1_done, 1)
                    if s == 4 and exists(b + 2):
                        wait(dve, rstd1_done, b + 3)
                        V.tensor_scalar(xin[e][:, :], xin[e][:, :], mv1[:, 0:1], rstd1[:, :], ALU.subtract,
                                        ALU.mult).then_inc(xn_done, 1)
                    if (s == S_OT1 + 1 and exists(b - 1)) or (s == S_OT0 + 1 and exists(b)):
                        ob, g = (b - 1, 1) if s == S_OT1 + 1 else (b, 0)
                        wait(dve, oT_ready, 2 * ob + g + 1)
                        wait(dve, o_tok_done, 2 * (ob - 1) + g + 1)
                        V.reciprocal(rec[:, g, :], misc[:, HD::2 * HD]).then_inc(rec_done, 1)
                        wait(dve, rec_done, 2 * ob + g + 1)
                        wait(dve, ob_ready, ob)
                        sums = misc[:, :].rearrange("p (t j c) -> p t j c", t=TT, c=2 * HD)[:, :, :, 0:HD]
                        V.tensor_tensor(o_tok[:, :, 64 * g:64 * g + 64].rearrange("p t (j c) -> p t j c", c=HD), sums,
                                        rec[:, g, :].rearrange("p (t j) -> p t j", t=TT).unsqueeze(3)
                                        .to_broadcast([P, TT, GROUP, HD]), ALU.mult).then_inc(o_tok_done, 1)
                    if s == S_WO + 2 and exists(b - 1):
                        wait(dve, attn_done, b)
                        wait(dve, xres_loaded[1 - e], 16 * (p + 1 if e else p))
                        wait(dve, x1_moved, 16 * (p if e else p - 1), 16 * PAIRS)
                        V.tensor_tensor(x1[:, 1 - e, :], attn[:, :], xres[1 - e][:, :], ALU.add).then_inc(x1_done, 1)
                        wait(dve, x1_done, b)
                        wait(dve, rstd2_step, 3 * (b - 1))
                        V.bn_stats(stats2[:, :], x1[:, 1 - e, :]).then_inc(bn2_done, 1)
                        wait(dve, bn2_done, b)
                        carry_wait(dve)
                        V.bn_aggr(mv2[:, :], stats2[:, :]).then_inc(mv2_done, 1)
                    if s == S_WO + 4 and exists(b - 1):
                        wait(dve, rstd2_step, 3 * b)
                        wait(dve, xlo_done, b - 1)
                        V.tensor_scalar(xn2[:, :], x1[:, 1 - e, :], mv2[:, 0:1], rstd2s[:, :], ALU.subtract,
                                        ALU.mult).then_inc(xn2_done, 1)
                        wait(dve, xn2_done, b)
                        wait(dve, xT_ready, b - 2)
                        V.tensor_copy(x_hl[1 - e][:, 0, :], xn2[:, :]).then_inc(xhi_done, 1)
                    if s == S_QPROJ + 2 and exists(b + 2):
                        wait(dve, qb_done, b + 3)
                        wait(dve, rope_q, 3 * (b + 2))
                        carry_wait(dve)
                        V.stream_shuffle(rq[:, :], qb[:, :], swap).then_inc(rq_done, 1)
                    if s == S_KPROJ + 2 and exists(b + 2):
                        wait(dve, kb_done, b + 3)
                        wait(dve, rope_k, 3 * (b + 2))
                        carry_wait(dve)
                        V.stream_shuffle(rk[:, :], kb[:, :], swap).then_inc(rk_done, 1)
                    if s == S_VPROJ + 1 and exists(b + 1):
                        wait(dve, v_ready, b + 2)
                        wait(dve, pv_done, QUADS * b)
                        V.tensor_tensor(v_sb[1 - e][:, :, :, 0:HD],
                                        misc[:, :].rearrange("p (t h c) -> p t h c", t=TT, c=HD),
                                        bv_sb.rearrange("p (h c) -> p h c", c=HD).unsqueeze(1)
                                        .to_broadcast([P, TT, HEADS, HD]), ALU.add).then_inc(v_done, 1)
                    if s == 18 and exists(b + 2):
                        wait(dve, rope_q, 3 * (b + 3))
                        wait(dve, scr_written, 32 * (b + 2))
                        V.tensor_copy(q_hl[:, 0, :], qb[:, :]).then_inc(qhi_done, 1)
                    if s == 21 and exists(b + 2):
                        wait(dve, rope_k, 3 * (b + 3))
                        V.tensor_copy(k_hl[:, 0, :], kb[:, :]).then_inc(khi_done, 1)
                    t = ffn_tile_at(S - 1)
                    if t is not None and exists(p - 1, PAIRS):
                        n = ET * (p - 1) + t
                        wait(dve, tanh_done, n + 1)
                        wait(dve, hb_done, n)
                        V.scalar_tensor_tensor(out=hu, in0=th[:, t % 2, :], scalar=1.0,
                                               in1=ff_ps[t % 2][:, 0:256], op0=ALU.add, op1=ALU.mult).then_inc(hu_done, 1)
                        wait(dve, hu_done, n + 1)
                        wait(dve, hlo_done, n - 1)
                        V.scalar_tensor_tensor(out=hb[:, t % 2, :], in0=hu, scalar=1.0 / (XN_SCALE * XN_SCALE * HID_SCALE),
                                               in1=ff_ps[t % 2][:, 256:512], op0=ALU.mult, op1=ALU.mult).then_inc(hb_done, 1)
                        wait(dve, hb_done, n + 1)
                        if t == 0:
                            wait(dve, y_ready, 2 * (p - 1))
                        V.tensor_copy(hid[:, t, 0, :], hb[:, t % 2, :]).then_inc(hhi_done, 1)
                    if e == 0 and s in (S_DOWN + 8, S_DOWN + 16) and exists(p - 2, PAIRS):
                        i = 0 if s == S_DOWN + 8 else 1
                        wait(dve, y_ready, 2 * (p - 2) + i + 1)
                        wait(dve, x1_moved, 16 * (p - 1))
                        wait(dve, out_written[i], 16 * (p - 1))
                        V.scalar_tensor_tensor(out=y_out[:, i, :], in0=ff_ps[i][:, :], scalar=y_coef[:, :],
                                               in1=x1_res[:, i, :], op0=ALU.mult, op1=ALU.add).then_inc(y_done, 1)
                    for m in range(3):
                        if not isinstance(b, int):
                            continue
                        if (b, s) == W_SCALE_AT[m]:
                            weight_scale(m)
                            if m == 2:
                                ffn_constants()
                        at, first = W_QUANT_AT[m]
                        if b == at and first <= s < first + 8:
                            quantise(m, s - first)

            pairs(dve, iteration)

        @block.gpsimd
        def _(pool):
            G = nc.gpsimd
            G.memset(half_neg[:, :], -0.5).then_inc(consts_set, 1)
            G.memset(ones[:, :], 1.0).then_inc(consts_set, 1)
            G.memset(ident[:, :], 0.0).then_inc(ident_set, 1)
            G.memset(ident16[:, :], 0.0).then_inc(ident_set, 1)
            pool.wait_ge(ident_set, 2)
            for t in (ident, ident16):
                G.affine_select(out=t[:, :], in_=t[:, :], compare_op=ALU.not_equal, fill=1.0, base=0,
                                pattern=[[-1, P]], channel_multiplier=1).then_inc(consts_set, 1)
            for i in range(2):
                pool.wait_ge(consts_set, 4 + i)
                G.memset(k_st[i][SHIFT_ROW:SHIFT_ROW + 1, :, :], -SHIFT).then_inc(consts_set, 1)
            pool.wait_ge(consts_set, 6)
            for i in range(2):
                G.memset(v_sb[i][:, :, :, HD:2 * HD], 1.0).then_inc(v_ones, 1)

            def iteration(p, e):
                b = PAIR * p + e
                for s in range(TILES):
                    S = TILES * e + s
                    if s == 1 and exists(b + 2):
                        wait(pool, mv1_done, b + 3)
                        wait(pool, rstd1_done, b + 2)
                        carry_wait(pool)
                        G.tensor_scalar(ve1[:, :], mv1[:, 1:2], LN_EPS, None, ALU.add).then_inc(ve1_done, 1)
                        wait(pool, ve1_done, b + 3)
                        wait(pool, xn_done, b + 2)
                        G.tensor_tensor(rstd1[:, :], ve1[:, :], half_neg[:, :], ALU.pow).then_inc(rstd1_done, 1)
                    if s == S_WO + 3 and exists(b - 1):
                        wait(pool, mv2_done, b)
                        carry_wait(pool)
                        G.tensor_scalar(ve2[:, :], mv2[:, 1:2], LN_EPS, None, ALU.add).then_inc(rstd2_step, 1)
                        wait(pool, rstd2_step, 3 * (b - 1) + 1)
                        G.tensor_tensor(rstd2[:, :], ve2[:, :], half_neg[:, :], ALU.pow).then_inc(rstd2_step, 1)
                        wait(pool, rstd2_step, 3 * (b - 1) + 2)
                        wait(pool, xn2_done, b - 1)
                        carry_wait(pool)
                        G.tensor_scalar(rstd2s[:, :], rstd2[:, :], XN_SCALE, None, ALU.mult).then_inc(rstd2_step, 1)
                    if s == S_WO + 5 and exists(b - 1):
                        wait(pool, xhi_done, b)
                        G.tensor_tensor(x_hl[1 - e][:, 1, :], xn2[:, :], x_hl[1 - e][:, 0, :],
                                        ALU.subtract).then_inc(xlo_done, 1)
                    for s0, src, turned, turned_done, steps in ((15, qb, rq, rq_done, rope_q), (18, kb, rk, rk_done, rope_k)):
                        if s == s0 and exists(b + 2):
                            wait(pool, turned_done, b + 3)
                            if is_at(b, -2):
                                pool.wait_ge(tables_loaded, 16)
                            G.tensor_tensor(src[:, :], src[:, :], cos_sb, ALU.mult).then_inc(steps, 1)
                        if s == s0 + 1 and exists(b + 2):
                            G.tensor_tensor(turned[:, :], turned[:, :], sin_sb, ALU.mult).then_inc(steps, 1)
                        if s == s0 + 2 and exists(b + 2):
                            wait(pool, steps, 3 * (b + 2) + 2)
                            G.tensor_tensor(src[:, :], src[:, :], turned[:, :], ALU.add).then_inc(steps, 1)
                    if s == 21 and exists(b + 2):
                        wait(pool, qhi_done, b + 3)
                        G.tensor_tensor(q_hl[:, 1, :], qb[:, :], q_hl[:, 0, :], ALU.subtract).then_inc(qlo_done, 1)
                    if s == 22 and exists(b + 2):
                        wait(pool, khi_done, b + 3)
                        G.tensor_tensor(k_hl[:, 1, :], kb[:, :], k_hl[:, 0, :], ALU.subtract).then_inc(klo_done, 1)
                    t = ffn_tile_at(S - 1)
                    if t is not None and exists(p - 1, PAIRS):
                        wait(pool, hhi_done, ET * (p - 1) + t + 1)
                        G.tensor_tensor(hid[:, t, 1, :], hb[:, t % 2, :], hid[:, t, 0, :],
                                        ALU.subtract).then_inc(hlo_done, 1)

            pairs(pool, iteration)

        @block.sync
        def _(sp):
            def wait(eng, s, value, total=None):
                if isinstance(value, int):
                    if total is not None:
                        value = min(value, total)
                    if value <= 0:
                        return
                eng.wait_ge(s, value)
                if not isinstance(value, int):
                    carry_wait(eng)

            def row(t, b):
                if isinstance(b, int):
                    return t[b, :, :]
                return t[bass.ds(sp.snap(b), 1), :, :].rearrange("a c t -> (a c) t")

            sp.dma_start(xin[0][:, :], x[0, :, :]).then_inc(xin_loaded[0], 16)
            for i in range(PAIR):
                sp.sem_inc(out_written[i], 16)
            sp.dma_start(small[:, :], attn_weights).then_inc(small_loaded, 16)
            sp.dma_start(cin[0][:, :], ctxt[0, :, :]).then_inc(cin_loaded[0], 16)
            sp.dma_start(tables[:, :, :], rotary).then_inc(tables_loaded, 16)

            def iteration(p, e):
                b = PAIR * p + e
                x_now = row(x, b) if exists(b) else None
                x_next, c_next = (row(x, b + 3), row(ctxt, b + 3)) if exists(b + 3) else (None, None)
                outs = [row(out, PAIR * (p - 2) + i) for i in range(PAIR)] if e == 0 and exists(p - 2, PAIRS) else None
                if exists(b):
                    wait(sp, x1_done, b - 1)
                    sp.dma_start(xres[e][:, :], x_now).then_inc(xres_loaded[e], 16)
                if exists(b + 3):
                    wait(sp, q_ready, b + 2)
                    sp.dma_start(xin[1 - e][:, :], x_next).then_inc(xin_loaded[1 - e], 16)
                if e == 0 and exists(p - 2, PAIRS):
                    wait(sp, y_done, 2 * (p - 2) + 1)
                    sp.dma_start(outs[0], y_out[:, 0, :]).then_inc(out_written[0], 16)
                if exists(b):
                    wait(sp, max_row_done, 2 * b + 2)
                    wait(sp, st_ready, TILES * (b - 1))
                    sp.dma_start(q_st[e][SHIFT_ROW:SHIFT_ROW + 1, GROUP:HEADS, :].rearrange("p h (a t) -> p (h a) t", a=TT),
                                 max_row[1][:, :]).then_inc(row_loaded[1], 16)
                if e == 0 and exists(p - 2, PAIRS):
                    wait(sp, y_done, 2 * (p - 2) + 2)
                    sp.dma_start(outs[1], y_out[:, 1, :]).then_inc(out_written[1], 16)
                if exists(b + 3):
                    wait(sp, v_ready, b + 2)
                    sp.dma_start(cin[1 - e][:, :], c_next).then_inc(cin_loaded[1 - e], 16)
                if e == 0 and exists(p - 1, PAIRS):
                    wait(sp, x1_done, 2 * p)
                    wait(sp, y_done, 2 * (p - 1))
                    if is_at(p, 1):
                        sp.wait_ge(quant_done, 24)
                    sp.dma_start(x1_res, x1[:, :, :]).then_inc(x1_moved, 16)
                if exists(b + 1):
                    wait(sp, max_row_done, 2 * (b + 1) + 1)
                    sp.dma_start(q_st[1 - e][SHIFT_ROW:SHIFT_ROW + 1, 0:GROUP, :].rearrange("p h (a t) -> p (h a) t", a=TT),
                                 max_row[0][:, :]).then_inc(row_loaded[0], 16)
                if exists(b + 2):
                    wait(sp, st_loaded[1 - e], 128 * (p + 2 if e else p + 1))
                    wait(sp, qlo_done, b + 3)
                    sp.dma_start(q_scr.rearrange("l p t -> p l t"), q_hl[:, :, :]).then_inc(scr_written, 16)
                    wait(sp, klo_done, b + 3)
                    sp.dma_start(k_scr.rearrange("l p t -> p l t"), k_hl[:, :, :]).then_inc(scr_written, 16)
                    wait(sp, st_ready, TILES * (b + 1))
                    wait(sp, scr_written, 32 * (b + 3))
                    for l in range(2):
                        for r in range(2):
                            qr, kr = 32 * r + 16 * l, 32 * l + 16 * r
                            sp.dma_start(q_st[e][qr:qr + HD, :, :],
                                         q_scr[l, :, :].rearrange("(h c) t -> c h t", c=HD)).then_inc(st_loaded[e], 16)
                            sp.dma_start(k_st[e][kr:kr + HD, :, :],
                                         k_scr[l, :, :].rearrange("(h c) t -> c h t", c=HD)).then_inc(st_loaded[e], 16)

            pairs(sp, iteration, last=PAIRS - 3)
            for i in range(PAIR):
                sp.wait_ge(out_written[i], 16 * (PAIRS + 1))


def _tables():
    inv = (np.float32(1.0) / np.float32(10000.0) ** (np.arange(0, HD, 2, dtype=np.float32) / np.float32(HD))).astype(np.float32)
    f = np.arange(SEQ, dtype=np.float32)[:, None] * inv[None, :]
    f = np.concatenate([f, f], axis=-1).astype(np.float32)
    sign = np.where(np.arange(HD) < HD // 2, np.float32(-1.0), np.float32(1.0))
    cos = np.tile(np.cos(f).T, (HEADS, 1)).astype(np.float32)
    sin = np.tile((np.sin(f) * sign[None, :]).T, (HEADS, 1)).astype(np.float32)
    return np.ascontiguousarray(np.stack([cos, sin], axis=1))


def kernel(x, ctx_2048, g_xattn, g_ffn, L0_xattn_Wq, L0_xattn_bq, L0_xattn_Wk, L0_xattn_bk, L0_xattn_Wv,
           L0_xattn_bv, L0_xattn_Wo, L0_xattn_bo, L0_ffn_W_up, L0_ffn_W_gate, L0_ffn_W_down):
    import concourse.bacc as _bacc
    from concourse.bass_utils import run_bass_kernel_spmd as _run

    a = np.asarray

    def tiles(w):
        w = a(w).T
        return np.ascontiguousarray(w.reshape(w.shape[0] // P, P, w.shape[1]).transpose(1, 0, 2)).reshape(P, -1)

    def columns(v, n):
        return np.broadcast_to(a(v)[None, :], (P, n))

    attn_weights = np.concatenate(
        [a(L0_xattn_Wq).T, a(L0_xattn_Wk).T, a(L0_xattn_Wv).T, a(L0_xattn_Wo).T, columns(L0_xattn_bv, CH),
         a(L0_xattn_bq)[:, None], a(L0_xattn_bk)[:, None], a(L0_xattn_bo)[:, None],
         columns(g_xattn, 1), columns(g_ffn, 1)], axis=1)
    ins = {
        "x": a(x), "ctxt": a(ctx_2048), "attn_weights": attn_weights, "rotary": _tables(),
        "wupT": tiles(L0_ffn_W_up), "wgateT": tiles(L0_ffn_W_gate), "wdownT": tiles(L0_ffn_W_down),
    }
    nc = _bacc.Bacc("TRN2", target_bir_lowering=False, num_devices=1)
    arrays, args = {}, []
    for name, v in ins.items():
        v = np.ascontiguousarray(v)
        arrays[f"in_{name}"] = v
        args.append(nc.dram_tensor(f"in_{name}", v.shape, mybir.dt.from_np(v.dtype), kind="ExternalInput").ap())
    out = nc.dram_tensor("out_0", (BATCH, CH, SEQ), mybir.dt.float32, kind="ExternalOutput").ap()
    flamingo_block(nc, *args, out)
    r = _run(nc, [arrays], core_ids=[0])
    return r.results[0]["out_0"]
```

```python
import numpy as np
import concourse.bass as bass
from concourse import mybir
from contextlib import ExitStack

BATCH, CH, SEQ = 16, 128, 512
HEADS = 8
HD = CH // HEADS
EXPERT = 2048
P = 128
TT = SEQ // P
ET = EXPERT // P
GROUP = HEADS // 2
PAIR = 2
PAIRS = BATCH // PAIR
TILES = HEADS * TT
QUADS = TILES // GROUP
QK_SCALE = 16.0
SHIFT = QK_SCALE * QK_SCALE
XN_SCALE = 2048.0
HID_SCALE = 16.0
LAG = 7
SMALL = 5 * CH + 5
MAGIC = 1.5 * 2.0 ** 23
SHIFT_ROW = 96
TWO_MINUS_SHIFT = float(np.array([-SHIFT, -SHIFT], np.float16).view(np.float32)[0])
LN_EPS = 1e-5
TERNARY_EPS = 1e-8

S_OT1, S_OBACK, S_WO, S_ROW1 = 3, 5, 7, 9
S_QPROJ, S_KPROJ, S_VPROJ, S_XT0, S_XT1, S_OT0, S_ROW0 = 11, 13, 15, 17, 20, 23, 26
S_NORM_STATS, S_NORM = 1, 7
S_ROPE_Q, S_ROPE_K = 15, 16
S_Q_HIGH, S_K_HIGH, S_Q_LOW, S_K_LOW = 20, 24, 21, 22
S_O_COPY1, S_O_COPY0 = 1, 19
S_X1, S_RSTD2, S_XN2, S_X_LOW = 11, 10, 13, 11
S_Y0, S_Y1 = 10, 18
UP_ABS_AT = (("project", -2, 13), ("project", -2, 20), ("project", -2, 21), ("project", -1, 12), ("project", -1, 13),
             ("project", -1, 20), ("project", -1, 21), ("project", -1, 22))
W_ABS_AT = (None, ("rest", -1, 12, 2), ("all", 1, 17, 3))
W_SUM_AT = (("project", -1, 20), ("rest", -1, 28), ("all", 2, 11))
W_SCALE_AT = (("project", -1, 20), ("rest", -1, 29), ("all", 2, 12))
W_ROUND_AT = (("project", -1, 21, 0), ("all", 0, 2, 2), ("all", 3, 3, 1))
W_CLIP_AT = (("rest", -1, 2, 1), ("all", 0, 3, 4), ("all", 3, 4, 3))
W_LOAD_AT = (None, ("rest", -1, 1, 2), ("all", 1, 11, 3))
S_DOWN = 0
S_FFN = 23


def flamingo_block(nc, x, ctxt, attn_weights, rotary, wupT, wgateT, wdownT, out):
    f32, f16 = mybir.dt.float32, mybir.dt.float16
    ALU, ACT, AX = mybir.AluOpType, mybir.ActivationFunctionType, mybir.AxisListType

    ctx = ExitStack()
    with ctx:
        def sb(name, shape, dt=f32):
            return ctx.enter_context(nc.sbuf_tensor(name, shape, dt))

        def sem(name):
            return ctx.enter_context(nc.semaphore(name))

        arena = sb("arena", [P, 16384])
        stage_a = arena[:, 0:8192]
        stage_b = arena[:, 8192:16384]
        w_up = sb("w_up", [P, TT, EXPERT], f16)
        w_gate = sb("w_gate", [P, TT, EXPERT], f16)
        w_down = arena[:, 7680:11776].bitcast(f16).rearrange("p (t d) -> p t d", t=ET)
        hid = arena[:, 0:4096].bitcast(f16).rearrange("p (e l r) -> p e l r", e=ET, l=2)
        x1_res = arena[:, 4096:5120].rearrange("p (b t) -> p b t", b=PAIR)
        y_out = arena[:, 5120:6144].rearrange("p (b t) -> p b t", b=PAIR)
        xT = arena[:, 6144:7168].bitcast(f16).rearrange("p (t l r) -> p t l r", t=TT, l=2)
        hb = arena[:, 7168:7680].rearrange("p (b r) -> p b r", b=2)
        abs_scrap = arena[:, 5120:5632].bitcast(f16)

        q_st = [sb(f"q_st{i}", [P, HEADS, SEQ], f16) for i in range(2)]
        k_st = [sb(f"k_st{i}", [P, HEADS, SEQ], f16) for i in range(2)]
        probs = sb("probs", [P, 2 * GROUP, SEQ])
        xin = [sb(f"xin{i}", [P, SEQ]) for i in range(2)]
        cin = [sb(f"cin{i}", [P, SEQ]) for i in range(2)]
        xres = [sb(f"xres{i}", [P, SEQ]) for i in range(2)]
        tables = sb("tables", [P, 2, SEQ])
        cos_sb, sin_sb = tables[:, 0, :], tables[:, 1, :]
        qb, kb, rq, rk = (sb(n, [P, SEQ]) for n in ("qb", "kb", "rq", "rk"))
        q_hl, k_hl = sb("q_hl", [P, 2, SEQ], f16), sb("k_hl", [P, 2, SEQ], f16)
        v_sb = [sb(f"v_sb{i}", [P, TT, HEADS, 2 * HD]) for i in range(2)]
        o_raw = sb("o_raw", [P, 2, SEQ])
        o_tok = sb("o_tok", [P, TT, CH])
        o_ch = sb("o_ch", [P, SEQ])
        attn = sb("attn", [P, SEQ])
        th, hu = sb("th", [P, 2, 256]), sb("hu", [P, 256])
        x1 = sb("x1", [P, PAIR, SEQ])
        x_hl = [sb(f"x_hl{i}", [P, 2, SEQ], f16) for i in range(2)]
        small = sb("small", [P, SMALL])
        wq_sb, wk_sb, wv_sb, wo_sb, bv_sb = (small[:, CH * i:CH * (i + 1)] for i in range(5))
        biases = small[:, 5 * CH:5 * CH + 3]
        gates = small[:, 5 * CH + 3:5 * CH + 5]
        ident = sb("ident", [P, P])
        ident16 = sb("ident16", [P, P], f16)
        ones = sb("ones", [P, P])
        maxima = sb("maxima", [P, TILES])
        max16 = sb("max16", [P, TILES], f16)
        max_row = [sb(f"max_row{i}", [16, P], f16) for i in range(2)]
        rec = sb("rec", [P, 2, 16])
        stats1, mv1, stats2, mv2 = sb("stats1", [P, 6]), sb("mv1", [P, 2]), sb("stats2", [P, 6]), sb("mv2", [P, 2])
        ve1, rstd1, ve2, rstd2, rstd2s = (sb(n, [P, 1]) for n in ("ve1", "rstd1", "ve2", "rstd2", "rstd2s"))
        half_neg = sb("half_neg", [P, 1])
        tgate = sb("tgate", [P, 2])
        bq16, bk16, tbo = sb("bq16", [P, 1]), sb("bk16", [P, 1]), sb("tbo", [P, 1])
        asum = sb("asum", [P, 3, 8])
        wscale = sb("wscale", [P, 3])
        wsum = sb("wsum", [P, 3])
        winv = sb("winv", [P, 3])
        neg_magic = sb("neg_magic", [P, 1])
        up_half = sb("up_half", [P, 1])
        yc1, yc2, y_coef = sb("yc1", [P, 1]), sb("yc2", [P, 1]), sb("y_coef", [P, 1])

        q_scr = nc.dram_tensor("q_scr", [2, P, SEQ], f16, kind="Internal").ap()
        k_scr = nc.dram_tensor("k_scr", [2, P, SEQ], f16, kind="Internal").ap()

        def bank(name):
            return ctx.enter_context(nc.psum_tensor(name, [P, 512], f32))

        st_ps = [bank("st_ps0"), bank("st_ps1")]
        mx_ps = [bank("mx_ps0"), bank("mx_ps1")]
        pv_ps = bank("pv_ps")
        misc = bank("misc")
        ff_ps = [bank("ff_ps0"), bank("ff_ps1")]
        misc16 = misc[:, :].bitcast(f16)

        consts_set, ident_set = sem("consts_set"), sem("ident_set")
        small_loaded, tables_loaded, dve_small = sem("small_loaded"), sem("tables_loaded"), sem("dve_small")
        rows_zero, v_ones = sem("rows_zero"), sem("v_ones")
        gate_tanh = sem("gate_tanh")
        up_loaded, gate_loaded, down_loaded = ([sem(f"{n}_loaded{c}") for c in range(8)] for n in ("up", "gate", "down"))
        w_loaded = [up_loaded, gate_loaded, down_loaded]
        abs_done, wsum_ready, wscale_done, winv_done = (sem(n) for n in ("abs_done", "wsum_ready", "wscale_done", "winv_done"))
        rounded, quant_done = sem("rounded"), sem("quant_done")
        xin_loaded = [sem("xin_loaded0"), sem("xin_loaded1")]
        cin_loaded = [sem("cin_loaded0"), sem("cin_loaded1")]
        xres_loaded = [sem("xres_loaded0"), sem("xres_loaded1")]
        bn1_done, mv1_done, ve1_done, rstd1_done, xn_done = (sem(n) for n in ("bn1_done", "mv1_done", "ve1_done", "rstd1_done", "xn_done"))
        q_ready, k_ready, v_ready = sem("q_ready"), sem("k_ready"), sem("v_ready")
        qb_done, kb_done, v_done = sem("qb_done"), sem("kb_done"), sem("v_done")
        rq_done, rk_done = sem("rq_done"), sem("rk_done")
        rope_q, rope_k = sem("rope_q"), sem("rope_k")
        qhi_done, khi_done, qlo_done, klo_done = (sem(n) for n in ("qhi_done", "khi_done", "qlo_done", "klo_done"))
        q_written, k_written = sem("q_written"), sem("k_written")
        st_loaded = [sem("st_loaded0"), sem("st_loaded1")]
        mx_ready, mx_done, max16_done, maxT_ready, max_row_done = (sem(n) for n in ("mx_ready", "mx_done", "max16_done", "maxT_ready", "max_row_done"))
        row_loaded = [sem("row_loaded0"), sem("row_loaded1")]
        st_ready, exp_done, pv_done, o_copied = (sem(n) for n in ("st_ready", "exp_done", "pv_done", "o_copied"))
        oT_ready, rec_done, o_tok_done, ob_ready, o_ch_done = (sem(n) for n in ("oT_ready", "rec_done", "o_tok_done", "ob_ready", "o_ch_done"))
        wo_ready, attn_done, x1_done = sem("wo_ready"), sem("attn_done"), sem("x1_done")
        bn2_done, mv2_done, rstd2_step, xn2_done, xhi_done, xlo_done = (sem(n) for n in ("bn2_done", "mv2_done", "rstd2_step", "xn2_done", "xhi_done", "xlo_done"))
        xT_ready, xT_done = sem("xT_ready"), sem("xT_done")
        ug_ready, tanh_done, hu_done, hb_done, hhi_done, hlo_done = (sem(n) for n in ("ug_ready", "tanh_done", "hu_done", "hb_done", "hhi_done", "hlo_done"))
        x1_moved, y_ready, y_done = sem("x1_moved"), sem("y_ready"), sem("y_done")
        out_written = [sem("out_written0"), sem("out_written1")]
        passed = sem("passed")
        block = ctx.enter_context(nc.Block())

        def wait(eng, s, value, total=None):
            if isinstance(value, int):
                if total is not None:
                    value = min(value, total)
                if value <= 0:
                    return
            eng.wait_ge(s, value)

        def carry_wait(eng):
            eng.sem_inc(passed, 1)

        def exists(b, count=BATCH):
            return part[0] in ("rest", "all") and (not isinstance(b, int) or 0 <= b < count)

        def norm_of(b):
            return part[0] in ("norm", "all") and (not isinstance(b, int) or 0 <= b < BATCH)

        def front_of(b):
            return part[0] in ("project", "all") and (not isinstance(b, int) or 0 <= b < BATCH)

        part = ["all"]

        def is_at(b, n):
            return isinstance(b, int) and b == n

        def stands_at(b, s, at):
            return isinstance(b, int) and (part[0], b, s) == at

        def eighths_at(b, s, at):
            if at is None:
                return []
            where, b0, s0, every = at
            return [c for c in range(8)
                    if stands_at(b, s, (where, b0 + (s0 + every * c) // TILES, (s0 + every * c) % TILES))]

        def pairs(eng, iteration, last=PAIRS - 2):
            for first, e in (("rest", 0), ("norm", 0), ("norm", 1), ("project", 0), ("project", 1), ("rest", 1)):
                part[0] = first
                iteration(-1, e)
            part[0] = "all"
            for p in (0, 1):
                for e in range(PAIR):
                    iteration(p, e)
            with eng.Fori(2, last + 1) as p:
                for e in range(PAIR):
                    iteration(p, e)
            for p in range(last + 1, PAIRS + 2):
                for e in range(PAIR):
                    iteration(p, e)

        def up_gate_span(S):
            n = [min(max(16 * ET * k // (2 * TILES - 1 - S_FFN), 0), 16 * ET) for k in (S - S_FFN, S - S_FFN + 1)]
            return range(*n)

        def ffn_tile_at(S):
            done = [n // 16 for n in up_gate_span(S) if n % 16 == 15]
            return done[0] if done else None

        def staged_eighth(m, c):
            return (stage_a, stage_b, stage_b)[m][:, 1024 * c:1024 * c + 1024]

        def ternary_eighth(m, c):
            if m == 2:
                return w_down[:, 2 * c:2 * c + 2, :].rearrange("p t d -> p (t d)")
            return (w_up, w_gate)[m][:, c // 2, 1024 * (c % 2):1024 * (c % 2) + 1024]

        @block.tensor
        def _(pe):
            MM, TR = nc.tensor.matmul, nc.tensor.transpose

            def weight_sum(m):
                pe.wait_ge(consts_set, 2)
                pe.wait_ge(abs_done, 8 * (m + 1))
                if m:
                    pe.wait_ge(wscale_done, m)
                MM(ff_ps[0][:, 0:8], ones[:, :], asum[:, m, :], start=True, stop=True).then_inc(wsum_ready, 1)

            def iteration(p, e):
                b = PAIR * p + e
                for s in range(TILES):
                    S = TILES * e + s
                    if exists(b):
                        if s == 0:
                            wait(pe, row_loaded[0], 16 * (b + 1))
                        if s == TILES // 2:
                            wait(pe, row_loaded[1], 16 * (b + 1))
                        h, j = GROUP * (s // 16) + s % 4, (s % 16) // 4
                        wait(pe, exp_done, TILES * b + s - 1)
                        MM(st_ps[s % 2][:, :], k_st[e][0:SHIFT_ROW + 1, h, P * j:P * j + P], q_st[e][0:SHIFT_ROW + 1, h, :],
                           start=True, stop=True).then_inc(st_ready, 1)
                    mb, m = (b, s + TILES - LAG) if s < LAG else (b + 1, s - LAG)
                    me = e if s < LAG else 1 - e
                    if exists(mb):
                        if m == 0 and (is_at(mb, 0) or is_at(mb, 1)):
                            pe.wait_ge(consts_set, 6)
                            pe.wait_ge(rows_zero, 4)
                        if m == 0:
                            wait(pe, st_loaded[me], 128 * (p + 2 if e else p + 1))
                        h, j = m // TT, m % TT
                        wait(pe, mx_done, TILES * mb + m - 1)
                        MM(mx_ps[m % 2][:, :], q_st[me][0:SHIFT_ROW, h, P * j:P * j + P],
                           k_st[me][0:SHIFT_ROW, h, :], start=True, stop=True).then_inc(mx_ready, 1)
                    qb_, k = (b, (s - 5) // 4) if s >= 5 else (b - 1, QUADS - 1)
                    if s % 4 == 1 and exists(qb_):
                        ve = e if s >= 5 else 1 - e
                        g, j = k // 4, k % 4
                        wait(pe, exp_done, TILES * qb_ + 4 * k + 4)
                        if k == 0:
                            wait(pe, v_done, qb_ + 1)
                            if is_at(qb_, 0):
                                pe.wait_ge(v_ones, 2)
                        if k % 4 == 0:
                            wait(pe, o_copied, 2 * qb_ + g)
                        for a in range(GROUP):
                            mm = MM(pv_ps[32 * a:32 * a + 32, :], v_sb[ve][:, j, GROUP * g + a, :],
                                    probs[:, (4 * k + a) % 8, :], start=(j == 0), stop=(j == TT - 1))
                        mm.then_inc(pv_done, 1)
                    if exists(p - 1, PAIRS):
                        for n in up_gate_span(S):
                            t, r = n // 16, n % 16
                            if n == 0:
                                wait(pe, xT_done, 2 * p)
                                if is_at(p, 1):
                                    pe.wait_ge(quant_done, 16)
                                    pe.wait_ge(wscale_done, 3)
                            if n == 0:
                                wait(pe, y_done, 2 * (p - 1) - 1)
                            if n == 16:
                                wait(pe, y_done, 2 * (p - 1))
                            if r == 0:
                                wait(pe, hb_done, ET * (p - 1) + t - 1)
                            w, c = (w_up, 0) if r < 8 else (w_gate, 256)
                            k, hl = (r % 8) // 2, r % 2
                            mm = MM(ff_ps[t % 2][:, c:c + 256], w[:, k, P * t:P * t + P], xT[:, k, hl, :],
                                    start=(r % 8 == 0), stop=(r % 8 == 7))
                            if r == 15:
                                mm.then_inc(ug_ready, 1)
                    if exists(p - 2, PAIRS) and S_DOWN <= S < S_DOWN + 16:
                        for n in range(4 * (S - S_DOWN), 4 * (S - S_DOWN) + 4):
                            i, t, hl = n // 32, (n % 32) // 2, n % 2
                            if n == 0:
                                pe.wait_ge(quant_done, 24)
                            if n % 32 == 0:
                                wait(pe, hb_done, ET * (p - 1) - 1 + i)
                            if i == 0 and hl == 0:
                                wait(pe, hlo_done, ET * (p - 2) + t + 1)
                            mm = MM(ff_ps[i][:, :], hid[:, t, hl, P * i:P * i + P], w_down[:, t, :],
                                    start=(n % 32 == 0), stop=(n % 32 == 31))
                        if n % 32 == 31:
                            mm.then_inc(y_ready, 1)
                    if (s == S_OT1 and exists(b - 1)) or (s == S_OT0 and exists(b)):
                        ob, g = (b - 1, 1) if s == S_OT1 else (b, 0)
                        wait(pe, o_copied, 2 * ob + g + 1)
                        if g:
                            wait(pe, o_tok_done, 2 * ob + g)
                            wait(pe, max_row_done, 2 * (ob + 1) + 1, 2 * BATCH)
                        else:
                            wait(pe, v_done, b + 2, BATCH)
                            wait(pe, attn_done, b)
                            if e == 0:
                                wait(pe, xT_done, 2 * p)
                        for j in range(TT):
                            mm = TR(misc[:, P * j:P * j + P], o_raw[:, g, P * j:P * j + P], ident[:, :])
                        mm.then_inc(oT_ready, 1)
                    if s == S_OBACK and exists(b - 1):
                        wait(pe, o_tok_done, 2 * b)
                        for j in range(TT):
                            mm = TR(misc[:, P * j:P * j + P], o_tok[:, j, :], ident[:, :])
                        mm.then_inc(ob_ready, 1)
                    if (s == S_ROW1 and exists(b)) or (s == S_ROW0 and exists(b + 1)):
                        rb, half = (b, 1) if s == S_ROW1 else (b + 1, 0)
                        wait(pe, max16_done, 2 * rb + half + 1)
                        if half:
                            wait(pe, attn_done, b)
                            wait(pe, max_row_done, 2 * b + 1)
                        else:
                            wait(pe, o_tok_done, 2 * b + 1)
                            wait(pe, v_done, b + 2, BATCH)
                        TR(misc16[0:16, 0:P], max16[:, 16 * half:16 * half + 16], ident16[:, :]).then_inc(maxT_ready, 1)
                    if s == S_WO and exists(b - 1):
                        wait(pe, o_ch_done, b)
                        MM(misc[:, :], wo_sb, o_ch[:, :], start=True, stop=True).then_inc(wo_ready, 1)
                    if s == S_QPROJ and front_of(b + 2):
                        if is_at(b, -2):
                            pe.wait_ge(small_loaded, 16)
                        wait(pe, xn_done, b + 3)
                        if is_at(b, -1):
                            pe.wait_ge(kb_done, 1)
                        wait(pe, attn_done, b)
                        wait(pe, max_row_done, 2 * b + 2, 2 * BATCH)
                        MM(misc[:, :], wq_sb, xin[e][:, :], start=True, stop=True).then_inc(q_ready, 1)
                    if s == S_KPROJ and front_of(b + 2):
                        wait(pe, cin_loaded[e], 16 * (p + 2))
                        wait(pe, qb_done, b + 3)
                        MM(misc[:, :], wk_sb, cin[e][:, :], start=True, stop=True).then_inc(k_ready, 1)
                    if s == S_VPROJ and exists(b + 1):
                        wait(pe, kb_done, b + 3, BATCH)
                        wait(pe, attn_done, b)
                        wait(pe, max_row_done, 2 * b + 2, 2 * BATCH)
                        for j in range(TT):
                            mm = MM(misc[:, P * j:P * j + P], cin[1 - e][:, P * j:P * j + P], wv_sb,
                                    start=True, stop=True)
                        mm.then_inc(v_ready, 1)
                    if e == 0 and s in (S_XT0, S_XT1) and exists(p - 1, PAIRS):
                        i = 0 if s == S_XT0 else 1
                        wait(pe, xlo_done, 2 * (p - 1) + i + 1)
                        wait(pe, v_done, b + 2, BATCH)
                        wait(pe, attn_done, b)
                        if i:
                            wait(pe, xT_done, 2 * (p - 1) + 1)
                        for k in range(TT):
                            for hl in range(2):
                                c = P * (2 * k + hl)
                                mm = TR(misc16[:, c:c + P], x_hl[i][:, hl, P * k:P * k + P], ident16[:, :])
                        mm.then_inc(xT_ready, 1)
                    for m, at in enumerate(W_SUM_AT):
                        if stands_at(b, s, at):
                            weight_sum(m)

            pairs(pe, iteration)

        @block.scalar
        def _(act):
            def load_eighth(m, c):
                act.dma_start(staged_eighth(m, c),
                              (wupT, wgateT, wdownT)[m][:, 1024 * c:1024 * c + 1024]).then_inc(w_loaded[m][c], 16)

            act.wait_ge(small_loaded, 16)
            nc.scalar.activation(tgate[:, :], gates, ACT.Tanh).then_inc(gate_tanh, 1)
            act.wait_ge(cin_loaded[0], 16)
            for c in range(8):
                load_eighth(0, c)

            def abs_rows(m, c):
                act.wait_ge(w_loaded[m][c], 16)
                if m == 2 and c:
                    act.wait_ge(abs_done, 8 * m + c)
                nc.scalar.activation(abs_scrap if m == 2 else ternary_eighth(m, c), staged_eighth(m, c), ACT.Abs,
                                     accum_out=asum[:, m, c:c + 1]).then_inc(abs_done, 1)

            def clip(m, c):
                act.wait_ge(rounded, 8 * m + c + 1)
                act.wait_ge(abs_done, 8 * m + c + 1)
                nc.scalar.activation(ternary_eighth(m, c), staged_eighth(m, c), ACT.Sign,
                                     bias=neg_magic[:, :]).then_inc(quant_done, 1)

            def iteration(p, e):
                b = PAIR * p + e
                for s in range(TILES):
                    S = TILES * e + s
                    t = ffn_tile_at(S - 1)
                    if t is not None and exists(p - 1, PAIRS):
                        wait(act, ug_ready, ET * (p - 1) + t + 1)
                        wait(act, hu_done, ET * (p - 1) + t - 1)
                        nc.scalar.activation(th[:, t % 2, :], ff_ps[t % 2][:, 0:256], ACT.Tanh,
                                             scale=up_half[:, :]).then_inc(tanh_done, 1)
                    if exists(b):
                        wait(act, st_ready, TILES * b + s + 1)
                        if s % 4 == 0:
                            wait(act, pv_done, QUADS * b + s // 4 - 1)
                        nc.scalar.activation(probs[:, s % 8, :], st_ps[s % 2][:, :], ACT.Exp,
                                             scale=1.0 / (SHIFT * float(HD) ** 0.5)).then_inc(exp_done, 1)
                    if (s == S_O_COPY1 and exists(b - 1)) or (s == S_O_COPY0 and exists(b)):
                        ob, g = (b - 1, 1) if s == S_O_COPY1 else (b, 0)
                        wait(act, pv_done, QUADS * ob + 4 * g + 4)
                        wait(act, oT_ready, 2 * (ob - 1) + g + 1)
                        nc.scalar.activation(o_raw[:, g, :], pv_ps[:, :], ACT.Copy).then_inc(o_copied, 1)
                    if s == S_OBACK + 1 and exists(b - 1):
                        wait(act, ob_ready, b)
                        wait(act, wo_ready, b - 1)
                        nc.scalar.activation(o_ch[:, :], misc[:, :], ACT.Copy).then_inc(o_ch_done, 1)
                    if s == S_WO + 1 and exists(b - 1):
                        wait(act, wo_ready, b)
                        wait(act, xlo_done, b - 1)
                        nc.scalar.activation(attn[:, :], misc[:, :], ACT.Identity, bias=tbo[:, :],
                                             scale=tgate[:, 0:1]).then_inc(attn_done, 1)
                    if e == 0 and s in (S_XT0 + 1, S_XT1 + 1) and exists(p - 1, PAIRS):
                        i = 0 if s == S_XT0 + 1 else 1
                        wait(act, xT_ready, 2 * (p - 1) + i + 1)
                        wait(act, ug_ready, ET * (p - 1))
                        if is_at(p, 1):
                            act.wait_ge(quant_done, 8)
                        nc.scalar.activation(xT[:, :, :, P * i:P * i + P],
                                             misc16.rearrange("p (t l r) -> p t l r", t=TT, l=2),
                                             ACT.Copy).then_inc(xT_done, 1)
                    if s == S_QPROJ + 1 and front_of(b + 2):
                        wait(act, q_ready, b + 3)
                        wait(act, qlo_done, b + 2)
                        if is_at(b, -2):
                            act.wait_ge(dve_small, 2)
                        nc.scalar.activation(qb[:, :], misc[:, :], ACT.Identity, bias=bq16[:, :],
                                             scale=QK_SCALE).then_inc(qb_done, 1)
                    if s == S_KPROJ + 1 and front_of(b + 2):
                        wait(act, k_ready, b + 3)
                        wait(act, klo_done, b + 2)
                        nc.scalar.activation(kb[:, :], misc[:, :], ACT.Identity, bias=bk16[:, :],
                                             scale=QK_SCALE).then_inc(kb_done, 1)
                    t = ffn_tile_at(S - 1)
                    if t is not None and exists(p - 1, PAIRS):
                        wait(act, hb_done, ET * (p - 1) + t + 1)
                        if t == 0:
                            wait(act, y_ready, 2 * (p - 1))
                        nc.scalar.activation(hid[:, t, 0, :], hb[:, t % 2, :], ACT.Copy).then_inc(hhi_done, 1)
                    for c, at in enumerate(UP_ABS_AT):
                        if stands_at(b, s, at):
                            abs_rows(0, c)
                    for m in range(3):
                        for c in eighths_at(b, s, W_ABS_AT[m]):
                            abs_rows(m, c)
                        for c in eighths_at(b, s, W_CLIP_AT[m]):
                            clip(m, c)
                    for m in (1, 2):
                        for c in eighths_at(b, s, W_LOAD_AT[m]):
                            if c == 0 and m == 1:
                                act.wait_ge(st_loaded[0], 128)
                            if c == 0 and m == 2:
                                act.wait_ge(quant_done, 16)
                            load_eighth(m, c)

            pairs(act, iteration)

        @block.vector
        def _(dve):
            V = nc.vector
            V.memset(neg_magic[:, :], -MAGIC).then_inc(dve_small, 1)
            dve.wait_ge(small_loaded, 16)
            V.tensor_scalar(bq16[:, :], biases[:, 0:1], QK_SCALE, None, ALU.mult)
            V.tensor_scalar(bk16[:, :], biases[:, 1:2], QK_SCALE, None, ALU.mult).then_inc(dve_small, 1)
            dve.wait_ge(gate_tanh, 1)
            V.tensor_scalar(tbo[:, :], biases[:, 2:3], tgate[:, 0:1], None, ALU.mult).then_inc(dve_small, 1)

            def weight_scale(m):
                dve.wait_ge(wsum_ready, m + 1)
                V.reduce_sum(wsum[:, m:m + 1], ff_ps[0][:, 0:8], axis=AX.X).then_inc(wscale_done, 1)
                dve.wait_ge(wscale_done, m + 1)
                V.tensor_scalar(wscale[:, m:m + 1], wsum[:, m:m + 1], 1.0 / (EXPERT * SEQ), TERNARY_EPS,
                                ALU.mult, ALU.add).then_inc(dve_small, 1)
                dve.wait_ge(dve_small, 3 + m + 1)
                V.reciprocal(winv[:, m:m + 1], wscale[:, m:m + 1]).then_inc(winv_done, 1)
                if m == 0:
                    V.tensor_scalar(up_half[:, :], wscale[:, 0:1], 0.5 / XN_SCALE, None, ALU.mult)

            def round_eighth(m, c):
                dve.wait_ge(winv_done, m + 1)
                dve.wait_ge(abs_done, 8 * m + c + 1)
                V.tensor_scalar(staged_eighth(m, c), staged_eighth(m, c), winv[:, m:m + 1], MAGIC, ALU.mult,
                                ALU.add).then_inc(rounded, 1)

            def ffn_constants():
                V.tensor_tensor(yc1[:, :], wscale[:, 0:1], wscale[:, 1:2], ALU.mult).then_inc(dve_small, 1)
                dve.wait_ge(dve_small, 7)
                V.tensor_tensor(yc2[:, :], yc1[:, :], wscale[:, 2:3], ALU.mult).then_inc(dve_small, 1)
                dve.wait_ge(dve_small, 8)
                V.tensor_scalar(y_coef[:, :], yc2[:, :], tgate[:, 1:2], 0.5 * HID_SCALE, ALU.mult,
                                ALU.mult).then_inc(dve_small, 1)
                dve.wait_ge(dve_small, 9)

            swap = [(i + HD // 2) % HD + HD * (i // HD) for i in range(32)]

            def iteration(p, e):
                b = PAIR * p + e
                for s in range(TILES):
                    S = TILES * e + s
                    mb, m = (b, s + TILES - LAG) if s < LAG else (b + 1, s - LAG)
                    if exists(mb):
                        wait(dve, mx_ready, TILES * mb + m + 1)
                        if m == 0:
                            wait(dve, max16_done, 2 * mb)
                        V.reduce_max(maxima[:, m:m + 1], mx_ps[m % 2][:, :], axis=AX.X).then_inc(mx_done, 1)
                    t = ffn_tile_at(S - 1)
                    if t is not None and exists(p - 1, PAIRS):
                        n = ET * (p - 1) + t
                        wait(dve, tanh_done, n + 1)
                        wait(dve, hb_done, n)
                        V.scalar_tensor_tensor(out=hu[:, :], in0=th[:, t % 2, :], scalar=1.0,
                                               in1=ff_ps[t % 2][:, 0:256], op0=ALU.add, op1=ALU.mult).then_inc(hu_done, 1)
                        wait(dve, hu_done, n + 1)
                        wait(dve, hlo_done, n - 1)
                        V.scalar_tensor_tensor(out=hb[:, t % 2, :], in0=hu[:, :], scalar=1.0 / (XN_SCALE * XN_SCALE * HID_SCALE),
                                               in1=ff_ps[t % 2][:, 256:512], op0=ALU.mult, op1=ALU.mult).then_inc(hb_done, 1)
                    if (s == LAG - 1 and exists(b)) or (s == LAG + 15 and exists(b + 1)):
                        rb, half = (b, 1) if s == LAG - 1 else (b + 1, 0)
                        wait(dve, mx_done, TILES * rb + 16 * half + 16)
                        wait(dve, maxT_ready, 2 * rb + half - 1)
                        V.tensor_scalar(max16[:, 16 * half:16 * half + 16], maxima[:, 16 * half:16 * half + 16],
                                        1.0 / SHIFT, None, ALU.mult).then_inc(max16_done, 1)
                    if (s == S_ROW1 + 1 and exists(b)) or (s == S_ROW0 + 1 and exists(b + 1)):
                        rb, half = (b, 1) if s == S_ROW1 + 1 else (b + 1, 0)
                        wait(dve, maxT_ready, 2 * rb + half + 1)
                        wait(dve, row_loaded[half], 16 * rb)
                        V.tensor_copy(max_row[half][:, :], misc16[0:16, 0:P]).then_inc(max_row_done, 1)
                    if s == S_NORM_STATS and norm_of(b + 2):
                        wait(dve, xin_loaded[e], 16 * (p + 2))
                        wait(dve, ve1_done, b + 2)
                        V.bn_stats(stats1[:, :], xin[e][:, :]).then_inc(bn1_done, 1)
                        wait(dve, bn1_done, b + 3)
                        carry_wait(dve)
                        V.bn_aggr(mv1[:, :], stats1[:, :]).then_inc(mv1_done, 1)
                    if s == S_NORM and norm_of(b + 2):
                        wait(dve, rstd1_done, b + 3)
                        V.tensor_scalar(xin[e][:, :], xin[e][:, :], mv1[:, 0:1], rstd1[:, :], ALU.subtract,
                                        ALU.mult).then_inc(xn_done, 1)
                    if (s == S_OT1 + 1 and exists(b - 1)) or (s == S_OT0 + 1 and exists(b)):
                        ob, g = (b - 1, 1) if s == S_OT1 + 1 else (b, 0)
                        wait(dve, oT_ready, 2 * ob + g + 1)
                        wait(dve, o_tok_done, 2 * (ob - 1) + g + 1)
                        V.reciprocal(rec[:, g, :], misc[:, HD::2 * HD]).then_inc(rec_done, 1)
                        wait(dve, rec_done, 2 * ob + g + 1)
                        wait(dve, ob_ready, ob)
                        sums = misc[:, :].rearrange("p (t j c) -> p t j c", t=TT, c=2 * HD)[:, :, :, 0:HD]
                        V.tensor_tensor(o_tok[:, :, 64 * g:64 * g + 64].rearrange("p t (j c) -> p t j c", c=HD), sums,
                                        rec[:, g, :].rearrange("p (t j) -> p t j", t=TT).unsqueeze(3)
                                        .to_broadcast([P, TT, GROUP, HD]), ALU.mult).then_inc(o_tok_done, 1)
                    if s == S_X1 and exists(b - 1):
                        wait(dve, attn_done, b)
                        wait(dve, xres_loaded[1 - e], 16 * (p + 1 if e else p))
                        wait(dve, x1_moved, 16 * (p if e else p - 1), 16 * PAIRS)
                        V.tensor_tensor(x1[:, 1 - e, :], attn[:, :], xres[1 - e][:, :], ALU.add).then_inc(x1_done, 1)
                        wait(dve, x1_done, b)
                        wait(dve, rstd2_step, 3 * (b - 1))
                        V.bn_stats(stats2[:, :], x1[:, 1 - e, :]).then_inc(bn2_done, 1)
                        wait(dve, bn2_done, b)
                        carry_wait(dve)
                        V.bn_aggr(mv2[:, :], stats2[:, :]).then_inc(mv2_done, 1)
                    if s == S_XN2 and exists(b - 1):
                        wait(dve, rstd2_step, 3 * b)
                        wait(dve, xlo_done, b - 1)
                        V.tensor_scalar(attn[:, :], x1[:, 1 - e, :], mv2[:, 0:1], rstd2s[:, :], ALU.subtract,
                                        ALU.mult).then_inc(xn2_done, 1)
                        wait(dve, xn2_done, b)
                        wait(dve, xT_ready, b - 2)
                        V.tensor_copy(x_hl[1 - e][:, 0, :], attn[:, :]).then_inc(xhi_done, 1)
                    if s == S_QPROJ + 2 and front_of(b + 2):
                        wait(dve, qb_done, b + 3)
                        wait(dve, rope_q, 3 * (b + 2))
                        carry_wait(dve)
                        V.stream_shuffle(rq[:, :], qb[:, :], swap).then_inc(rq_done, 1)
                    if s == S_KPROJ + 2 and front_of(b + 2):
                        wait(dve, kb_done, b + 3)
                        wait(dve, rope_k, 3 * (b + 2))
                        carry_wait(dve)
                        V.stream_shuffle(rk[:, :], kb[:, :], swap).then_inc(rk_done, 1)
                    if s == S_VPROJ + 1 and exists(b + 1):
                        wait(dve, v_ready, b + 2)
                        wait(dve, pv_done, QUADS * b)
                        V.tensor_tensor(v_sb[1 - e][:, :, :, 0:HD],
                                        misc[:, :].rearrange("p (t h c) -> p t h c", t=TT, c=HD),
                                        bv_sb.rearrange("p (h c) -> p h c", c=HD).unsqueeze(1)
                                        .to_broadcast([P, TT, HEADS, HD]), ALU.add).then_inc(v_done, 1)
                    on_dve = is_at(b, -2) or is_at(b, -1)
                    k_on_dve = is_at(b, -2)
                    for s0, src, turned, turned_done, steps, here in (
                            (S_QPROJ + 2, qb, rq, rq_done, rope_q, on_dve), (S_KPROJ + 2, kb, rk, rk_done, rope_k, k_on_dve)):
                        if s == s0 and here and front_of(b + 2):
                            wait(dve, turned_done, b + 3)
                            if is_at(b, -2):
                                dve.wait_ge(tables_loaded, 16)
                            V.tensor_tensor(src[:, :], src[:, :], cos_sb, ALU.mult).then_inc(steps, 1)
                            V.tensor_tensor(turned[:, :], turned[:, :], sin_sb, ALU.mult).then_inc(steps, 1)
                            wait(dve, steps, 3 * (b + 2) + 2)
                            V.tensor_tensor(src[:, :], src[:, :], turned[:, :], ALU.add).then_inc(steps, 1)
                    if s == (S_QPROJ + 2 if on_dve else S_Q_HIGH) and front_of(b + 2):
                        wait(dve, rope_q, 3 * (b + 3))
                        wait(dve, q_written, 16 * (b + 2))
                        V.tensor_copy(q_hl[:, 0, :], qb[:, :]).then_inc(qhi_done, 1)
                        if on_dve:
                            wait(dve, qhi_done, b + 3)
                            V.tensor_tensor(q_hl[:, 1, :], qb[:, :], q_hl[:, 0, :],
                                            ALU.subtract).then_inc(qlo_done, 1)
                    if s == (S_KPROJ + 2 if k_on_dve else S_K_HIGH) and front_of(b + 2):
                        wait(dve, rope_k, 3 * (b + 3))
                        wait(dve, k_written, 16 * (b + 2))
                        V.tensor_copy(k_hl[:, 0, :], kb[:, :]).then_inc(khi_done, 1)
                        if k_on_dve:
                            wait(dve, khi_done, b + 3)
                            V.tensor_tensor(k_hl[:, 1, :], kb[:, :], k_hl[:, 0, :],
                                            ALU.subtract).then_inc(klo_done, 1)
                    if e == 0 and s in (S_Y0, S_Y1) and exists(p - 2, PAIRS):
                        i = 0 if s == S_Y0 else 1
                        wait(dve, y_ready, 2 * (p - 2) + i + 1)
                        wait(dve, x1_moved, 16 * (p - 1))
                        wait(dve, out_written[i], 16 * (p - 1))
                        V.scalar_tensor_tensor(out=y_out[:, i, :], in0=ff_ps[i][:, :], scalar=y_coef[:, :],
                                               in1=x1_res[:, i, :], op0=ALU.mult, op1=ALU.add).then_inc(y_done, 1)
                    for m in range(3):
                        if stands_at(b, s, W_SCALE_AT[m]):
                            weight_scale(m)
                            if m == 2:
                                ffn_constants()
                        for c in eighths_at(b, s, W_ROUND_AT[m]):
                            round_eighth(m, c)

            pairs(dve, iteration)

        @block.gpsimd
        def _(pool):
            G = nc.gpsimd
            G.memset(half_neg[:, :], -0.5).then_inc(consts_set, 1)
            def constants():
                G.memset(ones[:, :], 1.0).then_inc(consts_set, 1)
                G.memset(ident[:, :], 0.0).then_inc(ident_set, 1)
                G.memset(ident16[:, :], 0.0).then_inc(ident_set, 1)
                pool.wait_ge(ident_set, 2)
                for t in (ident, ident16):
                    G.affine_select(out=t[:, :], in_=t[:, :], compare_op=ALU.not_equal, fill=1.0, base=0,
                                    pattern=[[-1, P]], channel_multiplier=1).then_inc(consts_set, 1)
                for i in range(2):
                    pool.wait_ge(consts_set, 4 + i)
                    G.memset(k_st[i][SHIFT_ROW:SHIFT_ROW + 1, :, :].rearrange("p h t -> p (h t)").bitcast(f32),
                             TWO_MINUS_SHIFT).then_inc(consts_set, 1)
                pool.wait_ge(consts_set, 6)
                for i in range(2):
                    G.memset(v_sb[i][:, :, :, HD:2 * HD], 1.0).then_inc(v_ones, 1)
                pool.wait_ge(v_ones, 2)
                for i, t in enumerate((q_st[0], k_st[0], q_st[1], k_st[1])):
                    if i:
                        pool.wait_ge(rows_zero, i)
                    G.memset(t[64:SHIFT_ROW, :, :].rearrange("p h t -> p (h t)").bitcast(f32),
                             0.0).then_inc(rows_zero, 1)
                pool.wait_ge(rows_zero, 4)

            def iteration(p, e):
                b = PAIR * p + e
                for s in range(TILES):
                    S = TILES * e + s
                    if s == S_NORM_STATS and norm_of(b + 2):
                        wait(pool, mv1_done, b + 3)
                        wait(pool, rstd1_done, b + 2)
                        carry_wait(pool)
                        G.tensor_scalar(ve1[:, :], mv1[:, 1:2], LN_EPS, None, ALU.add).then_inc(ve1_done, 1)
                        wait(pool, ve1_done, b + 3)
                        wait(pool, xn_done, b + 2)
                        G.tensor_tensor(rstd1[:, :], ve1[:, :], half_neg[:, :], ALU.pow).then_inc(rstd1_done, 1)
                    if stands_at(b, s, ("norm", -1, 5)):
                        constants()
                    if s == S_RSTD2 and exists(b - 1):
                        wait(pool, mv2_done, b)
                        carry_wait(pool)
                        G.tensor_scalar(ve2[:, :], mv2[:, 1:2], LN_EPS, None, ALU.add).then_inc(rstd2_step, 1)
                        wait(pool, rstd2_step, 3 * (b - 1) + 1)
                        G.tensor_tensor(rstd2[:, :], ve2[:, :], half_neg[:, :], ALU.pow).then_inc(rstd2_step, 1)
                        wait(pool, rstd2_step, 3 * (b - 1) + 2)
                        wait(pool, xn2_done, b - 1)
                        carry_wait(pool)
                        G.tensor_scalar(rstd2s[:, :], rstd2[:, :], XN_SCALE, None, ALU.mult).then_inc(rstd2_step, 1)
                    if s == S_X_LOW and exists(b - 1):
                        wait(pool, xhi_done, b)
                        G.tensor_tensor(x_hl[1 - e][:, 1, :], attn[:, :], x_hl[1 - e][:, 0, :],
                                        ALU.subtract).then_inc(xlo_done, 1)
                    q_here = front_of(b + 2) and not (is_at(b, -2) or is_at(b, -1))
                    k_here = front_of(b + 2) and not is_at(b, -2)
                    for s0, src, turned, turned_done, steps, here in ((S_ROPE_Q, qb, rq, rq_done, rope_q, q_here),
                                                                      (S_ROPE_K, kb, rk, rk_done, rope_k, k_here)):
                        if s == s0 and here:
                            wait(pool, turned_done, b + 3)
                            if is_at(b, -1):
                                pool.wait_ge(tables_loaded, 16)
                            G.tensor_tensor(src[:, :], src[:, :], cos_sb, ALU.mult).then_inc(steps, 1)
                        if s == s0 + 1 and here:
                            G.tensor_tensor(turned[:, :], turned[:, :], sin_sb, ALU.mult).then_inc(steps, 1)
                        if s == s0 + 2 and here:
                            wait(pool, steps, 3 * (b + 2) + 2)
                            G.tensor_tensor(src[:, :], src[:, :], turned[:, :], ALU.add).then_inc(steps, 1)
                    if s == S_Q_LOW and q_here:
                        wait(pool, qhi_done, b + 3)
                        G.tensor_tensor(q_hl[:, 1, :], qb[:, :], q_hl[:, 0, :], ALU.subtract).then_inc(qlo_done, 1)
                    if s == S_K_LOW and k_here:
                        wait(pool, khi_done, b + 3)
                        G.tensor_tensor(k_hl[:, 1, :], kb[:, :], k_hl[:, 0, :], ALU.subtract).then_inc(klo_done, 1)
                    t = ffn_tile_at(S - 1)
                    if t is not None and exists(p - 1, PAIRS):
                        wait(pool, hhi_done, ET * (p - 1) + t + 1)
                        G.tensor_tensor(hid[:, t, 1, :], hb[:, t % 2, :], hid[:, t, 0, :],
                                        ALU.subtract).then_inc(hlo_done, 1)

            pairs(pool, iteration)

        @block.sync
        def _(sp):
            def wait(eng, s, value, total=None):
                if isinstance(value, int):
                    if total is not None:
                        value = min(value, total)
                    if value <= 0:
                        return
                eng.wait_ge(s, value)
                if not isinstance(value, int):
                    carry_wait(eng)

            def row(t, b):
                if isinstance(b, int):
                    return t[b, :, :]
                return t[bass.ds(sp.snap(b), 1), :, :].rearrange("a c t -> (a c) t")

            sp.dma_start(xin[0][:, :], x[0, :, :]).then_inc(xin_loaded[0], 16)
            for i in range(PAIR):
                sp.sem_inc(out_written[i], 16)
            sp.dma_start(small[:, :], attn_weights).then_inc(small_loaded, 16)
            sp.dma_start(cin[0][:, :], ctxt[0, :, :]).then_inc(cin_loaded[0], 16)
            sp.dma_start(tables[:, :, :], rotary).then_inc(tables_loaded, 16)

            def iteration(p, e):
                b = PAIR * p + e
                x_now = row(x, b) if exists(b) else None
                x_next, c_next = (row(x, b + 3), row(ctxt, b + 3)) if exists(b + 3) else (None, None)
                outs = [row(out, PAIR * (p - 2) + i) for i in range(PAIR)] if e == 0 and exists(p - 2, PAIRS) else None
                if exists(b):
                    wait(sp, x1_done, b - 1)
                    sp.dma_start(xres[e][:, :], x_now).then_inc(xres_loaded[e], 16)
                if exists(b + 3):
                    wait(sp, q_ready, b + 2)
                    sp.dma_start(xin[1 - e][:, :], x_next).then_inc(xin_loaded[1 - e], 16)
                if e == 0 and exists(p - 2, PAIRS):
                    wait(sp, y_done, 2 * (p - 2) + 1)
                    sp.dma_start(outs[0], y_out[:, 0, :]).then_inc(out_written[0], 16)
                if exists(b):
                    wait(sp, max_row_done, 2 * b + 2)
                    wait(sp, st_ready, TILES * (b - 1))
                    sp.dma_start(q_st[e][SHIFT_ROW:SHIFT_ROW + 1, GROUP:HEADS, :].rearrange("p h (a t) -> p (h a) t", a=TT),
                                 max_row[1][:, :]).then_inc(row_loaded[1], 16)
                if e == 0 and exists(p - 2, PAIRS):
                    wait(sp, y_done, 2 * (p - 2) + 2)
                    sp.dma_start(outs[1], y_out[:, 1, :]).then_inc(out_written[1], 16)
                if exists(b + 3):
                    wait(sp, v_ready, b + 2)
                    sp.dma_start(cin[1 - e][:, :], c_next).then_inc(cin_loaded[1 - e], 16)
                if e == 0 and exists(p - 1, PAIRS):
                    wait(sp, x1_done, 2 * p)
                    wait(sp, y_done, 2 * (p - 1))
                    if is_at(p, 1):
                        sp.wait_ge(quant_done, 8)
                    sp.dma_start(x1_res, x1[:, :, :]).then_inc(x1_moved, 16)
                if exists(b + 1):
                    wait(sp, max_row_done, 2 * (b + 1) + 1)
                    sp.dma_start(q_st[1 - e][SHIFT_ROW:SHIFT_ROW + 1, 0:GROUP, :].rearrange("p h (a t) -> p (h a) t", a=TT),
                                 max_row[0][:, :]).then_inc(row_loaded[0], 16)
                if front_of(b + 2):
                    wait(sp, st_loaded[1 - e], 128 * (p + 2 if e else p + 1))

                    def send(low_done, parts, scr, written):
                        wait(sp, low_done, b + 3)
                        sp.dma_start(scr.rearrange("l p t -> p l t"), parts[:, :, :]).then_inc(written, 16)

                    def fetch(scr, written, stack, row_of):
                        wait(sp, written, 16 * (b + 3))
                        for l in range(2):
                            for r in range(2):
                                sp.dma_start(stack[e][row_of(l, r):row_of(l, r) + HD, :, :],
                                             scr[l, :, :].rearrange("(h c) t -> c h t", c=HD)).then_inc(st_loaded[e], 16)

                    send(qlo_done, q_hl, q_scr, q_written)
                    send(klo_done, k_hl, k_scr, k_written)
                    wait(sp, st_ready, TILES * (b + 1))
                    fetch(q_scr, q_written, q_st, lambda l, r: 32 * r + 16 * l)
                    fetch(k_scr, k_written, k_st, lambda l, r: 32 * l + 16 * r)

            pairs(sp, iteration, last=PAIRS - 3)
            for i in range(PAIR):
                sp.wait_ge(out_written[i], 16 * (PAIRS + 1))


def _tables():
    inv = (np.float32(1.0) / np.float32(10000.0) ** (np.arange(0, HD, 2, dtype=np.float32) / np.float32(HD))).astype(np.float32)
    f = np.arange(SEQ, dtype=np.float32)[:, None] * inv[None, :]
    f = np.concatenate([f, f], axis=-1).astype(np.float32)
    sign = np.where(np.arange(HD) < HD // 2, np.float32(-1.0), np.float32(1.0))
    cos = np.tile(np.cos(f).T, (HEADS, 1)).astype(np.float32)
    sin = np.tile((np.sin(f) * sign[None, :]).T, (HEADS, 1)).astype(np.float32)
    return np.ascontiguousarray(np.stack([cos, sin], axis=1))


def kernel(x, ctx_2048, g_xattn, g_ffn, L0_xattn_Wq, L0_xattn_bq, L0_xattn_Wk, L0_xattn_bk, L0_xattn_Wv,
           L0_xattn_bv, L0_xattn_Wo, L0_xattn_bo, L0_ffn_W_up, L0_ffn_W_gate, L0_ffn_W_down):
    import concourse.bacc as _bacc
    from concourse.bass_utils import run_bass_kernel_spmd as _run

    a = np.asarray

    def tiles(w):
        w = a(w).T
        return np.ascontiguousarray(w.reshape(w.shape[0] // P, P, w.shape[1]).transpose(1, 0, 2)).reshape(P, -1)

    def columns(v, n):
        return np.broadcast_to(a(v)[None, :], (P, n))

    attn_weights = np.concatenate(
        [a(L0_xattn_Wq).T, a(L0_xattn_Wk).T, a(L0_xattn_Wv).T, a(L0_xattn_Wo).T, columns(L0_xattn_bv, CH),
         a(L0_xattn_bq)[:, None], a(L0_xattn_bk)[:, None], a(L0_xattn_bo)[:, None],
         columns(g_xattn, 1), columns(g_ffn, 1)], axis=1)
    ins = {
        "x": a(x), "ctxt": a(ctx_2048), "attn_weights": attn_weights, "rotary": _tables(),
        "wupT": tiles(L0_ffn_W_up), "wgateT": tiles(L0_ffn_W_gate), "wdownT": tiles(L0_ffn_W_down),
    }
    nc = _bacc.Bacc("TRN2", target_bir_lowering=False, num_devices=1)
    arrays, args = {}, []
    for name, v in ins.items():
        v = np.ascontiguousarray(v)
        arrays[f"in_{name}"] = v
        args.append(nc.dram_tensor(f"in_{name}", v.shape, mybir.dt.from_np(v.dtype), kind="ExternalInput").ap())
    out = nc.dram_tensor("out_0", (BATCH, CH, SEQ), mybir.dt.float32, kind="ExternalOutput").ap()
    flamingo_block(nc, *args, out)
    r = _run(nc, [arrays], core_ids=[0])
    return r.results[0]["out_0"]
```
